# Optimizing a Trainium2 kernel written in Bass

```python
import numpy as np
import jax
import jax.numpy as jnp

def _softmax(x, axis=-1):
    return jax.nn.softmax(x, axis=axis)

def _gelu(x):
    return jax.nn.gelu(x, approximate=True)

def _silu(x):
    return jax.nn.silu(x)

def _sigmoid(x):
    return jax.nn.sigmoid(x)

def _layernorm(x, axis=-1, eps=1e-05):
    m = jnp.mean(x, axis=axis, keepdims=True)
    v = jnp.var(x, axis=axis, keepdims=True)
    return (x - m) / jnp.sqrt(v + eps)

def _scatter_add(tgt, idx, src, axis=0):
    return tgt.at[idx].add(src)

def _segment_sum(src, seg, n):
    return jax.ops.segment_sum(src, seg, n)
kernel_name = 'mk_decoder_postln_d1_seqx_r8_976d02'

def setup_inputs(seed: int=0):
    np.random.seed(seed)
    _w = jnp.asarray

    def _rec_inputs():
        import jax
        import jax.numpy as jnp
        _rk = jax.random.key(seed)
        x = 0.5 + 0.2887 * jax.random.normal(jax.random.fold_in(_rk, 1), (4, 256, 256), jnp.float32)
        _lenS = 256 - jax.random.randint(jax.random.fold_in(_rk, 7), (4,), 0, max(1, 256 // 4) + 1, jnp.int32)
        _lenS2 = 256 - jax.random.randint(jax.random.fold_in(_rk, 8), (4,), 0, max(1, 256 // 4) + 1, jnp.int32)
        _ctx_512P = jax.random.normal(jax.random.fold_in(_rk, 11), (4, 16, 64), jnp.float32)
        _ctx_512c = jax.random.dirichlet(jax.random.fold_in(_rk, 511), 0.3 * jnp.ones((16,), jnp.float32), (4, 256))
        _ctx_512t = jnp.einsum('bsk,bkd->bsd', _ctx_512c, _ctx_512P)
        _ctx_512t = _ctx_512t * jax.lax.rsqrt(jnp.mean(jnp.square(_ctx_512t)) + 1e-12) * 0.953939
        ctx_512 = 7.22013e-05 + 1.00017 * (_ctx_512t + 0.3 * jax.random.normal(jax.random.fold_in(_rk, 611), (4, 256, 64), jnp.float32))
        _validS = jnp.arange(256)[None, :] < _lenS[:, None]
        _validS2 = jnp.arange(256)[None, :] < _lenS2[:, None]
        _causal = jnp.tril(jnp.ones((256, 256), dtype=bool))
        mask_SxS2_bk1 = jnp.broadcast_to(_validS2[0:1, :], (256, 256))
        mask_BxS2_bf0 = jnp.logical_not(jnp.ones((4, 256), dtype=bool))
        return (x, ctx_512, mask_SxS2_bk1, mask_BxS2_bf0)
    x, ctx_512, mask_SxS2_bk1, mask_BxS2_bf0 = _rec_inputs()

    def _L0_attn_setup():
        import jax, jax.numpy as jnp
        import numpy as np
        from jax import lax
        B_SZ, L, D_HID = (4, 512, 256)
        H, N, K, DT_RANK = (32, 16, 4, 128)
        D_INNER = H * N
        key = jax.random.key(seed)
        ks = jax.random.split(key, 12)
        s = 0.02
        inp = {'hidden_states': jax.random.normal(ks[0], (B_SZ, L, D_HID), jnp.float32), 'W_in_x': jax.random.normal(ks[1], (D_INNER, D_HID), jnp.float32) * s, 'W_in_z': jax.random.normal(ks[2], (D_INNER, D_HID), jnp.float32) * s, 'conv_w': jax.random.normal(ks[3], (D_INNER, 1, K), jnp.float32) * 0.1, 'conv_b': jax.random.normal(ks[4], (D_INNER,), jnp.float32) * 0.01, 'W_param': jax.random.normal(ks[5], (DT_RANK + 2 * H * N, D_INNER), jnp.float32) * s, 'W_dt': jax.random.normal(ks[6], (H, DT_RANK), jnp.float32) * s, 'b_dt': jnp.log(jax.random.uniform(ks[7], (H,), jnp.float32, 0.001, 0.01)), 'A_log': jnp.log(jax.random.uniform(ks[8], (H, N), jnp.float32, 0.1, 0.9)), 'D': jnp.ones((D_INNER,), jnp.float32), 'W_out': jax.random.normal(ks[9], (D_HID, D_INNER), jnp.float32) * s}
        return inp
    _L0_attn_all = _L0_attn_setup()
    _L0_attn_in = {k: v for k, v in _L0_attn_all.items() if k in ('W_in_x', 'W_in_z', 'conv_w', 'conv_b', 'W_param', 'W_dt', 'b_dt', 'A_log', 'D', 'W_out')}
    del _L0_attn_all

    def _L0_xattn_setup():
        import jax, jax.numpy as jnp
        import numpy as np
        B, S, H = (8, 256, 64)
        key = jax.random.key(seed)
        kq, kk, kqc, kwq, kwk = jax.random.split(key, 5)
        q = jax.random.normal(kq, (B, S, H), dtype=jnp.float32)
        k = jax.random.normal(kk, (B, S, H), dtype=jnp.float32)
        qc_score = jax.random.uniform(kqc, (B, S, S), dtype=jnp.float32)
        attn_mask = jnp.triu(jnp.ones((S, S), dtype=bool), k=1)
        key_padding_mask = jnp.zeros((B, S), dtype=bool)
        scale = 1.0 / np.sqrt(H)
        Wq = jax.random.normal(kwq, (H, H), dtype=jnp.float32) * scale
        Wk = jax.random.normal(kwk, (H, H), dtype=jnp.float32) * scale
        bq = jnp.zeros((H,), dtype=jnp.float32)
        bk = jnp.zeros((H,), dtype=jnp.float32)
        return {'q': q, 'k': k, 'attn_mask': attn_mask, 'key_padding_mask': key_padding_mask, 'qc_score': qc_score, 'Wq': Wq, 'bq': bq, 'Wk': Wk, 'bk': bk}
    _L0_xattn_all = _L0_xattn_setup()
    _L0_xattn_in = {k: v for k, v in _L0_xattn_all.items() if k in ('Wq', 'bq', 'Wk', 'bk')}
    del _L0_xattn_all

    def _L0_ffn_setup():
        import jax, jax.numpy as jnp
        import numpy as np
        HIDDEN = 256
        INTER = 688
        LUT_SIZE = 16

        def _ghost_linear(x, idx, lut):
            w = lut[idx]
            return jnp.einsum('bsh,oh->bso', x, w)
        key = jax.random.key(seed)
        k_x, k_lut, k_g, k_u, k_d = jax.random.split(key, 5)
        x = jax.random.normal(k_x, (2, 512, HIDDEN), dtype=jnp.float32)
        lut = jax.random.normal(k_lut, (LUT_SIZE,), dtype=jnp.float32) * 0.02
        gate_idx = jax.random.randint(k_g, (INTER, HIDDEN), 0, LUT_SIZE, dtype=jnp.int32)
        up_idx = jax.random.randint(k_u, (INTER, HIDDEN), 0, LUT_SIZE, dtype=jnp.int32)
        down_idx = jax.random.randint(k_d, (HIDDEN, INTER), 0, LUT_SIZE, dtype=jnp.int32)
        return {'x': x, 'lut': lut, 'gate_idx': gate_idx, 'up_idx': up_idx, 'down_idx': down_idx}
    _L0_ffn_all = _L0_ffn_setup()
    _L0_ffn_in = {k: v for k, v in _L0_ffn_all.items() if k in ('lut', 'gate_idx', 'up_idx', 'down_idx')}
    del _L0_ffn_all
    return {'x': x, 'ctx_512': ctx_512, 'mask_SxS2_bk1': mask_SxS2_bk1, 'mask_BxS2_bf0': mask_BxS2_bf0, 'L0_attn_W_in_x': _L0_attn_in['W_in_x'], 'L0_attn_W_in_z': _L0_attn_in['W_in_z'], 'L0_attn_conv_w': _L0_attn_in['conv_w'], 'L0_attn_conv_b': _L0_attn_in['conv_b'], 'L0_attn_W_param': _L0_attn_in['W_param'], 'L0_attn_W_dt': _L0_attn_in['W_dt'], 'L0_attn_b_dt': _L0_attn_in['b_dt'], 'L0_attn_A_log': _L0_attn_in['A_log'], 'L0_attn_D': _L0_attn_in['D'], 'L0_attn_W_out': _L0_attn_in['W_out'], 'L0_xattn_Wq': _L0_xattn_in['Wq'], 'L0_xattn_bq': _L0_xattn_in['bq'], 'L0_xattn_Wk': _L0_xattn_in['Wk'], 'L0_xattn_bk': _L0_xattn_in['bk'], 'L0_ffn_lut': _L0_ffn_in['lut'], 'L0_ffn_gate_idx': _L0_ffn_in['gate_idx'], 'L0_ffn_up_idx': _L0_ffn_in['up_idx'], 'L0_ffn_down_idx': _L0_ffn_in['down_idx']}

def reference(x, ctx_512, mask_SxS2_bk1, mask_BxS2_bf0, L0_attn_W_in_x, L0_attn_W_in_z, L0_attn_conv_w, L0_attn_conv_b, L0_attn_W_param, L0_attn_W_dt, L0_attn_b_dt, L0_attn_A_log, L0_attn_D, L0_attn_W_out, L0_xattn_Wq, L0_xattn_bq, L0_xattn_Wk, L0_xattn_bk, L0_ffn_lut, L0_ffn_gate_idx, L0_ffn_up_idx, L0_ffn_down_idx):
    import jax
    import jax.numpy as jnp

    def _L0_attn_ref(hidden_states, W_in_x, W_in_z, conv_w, conv_b, W_param, W_dt, b_dt, A_log, D, W_out):
        import jax, jax.numpy as jnp
        import numpy as np
        from jax import lax
        B_SZ, L, D_HID = (4, 512, 256)
        H, N, K, DT_RANK = (32, 16, 4, 128)
        D_INNER = H * N
        B, Lq, _ = hidden_states.shape
        x = hidden_states @ W_in_x.T
        z = hidden_states @ W_in_z.T
        xc = jnp.pad(x.transpose(0, 2, 1), ((0, 0), (0, 0), (K - 1, 0)))
        xconv = lax.conv_general_dilated(xc, conv_w, window_strides=(1,), padding='VALID', dimension_numbers=('NCH', 'OIH', 'NCH'), feature_group_count=D_INNER) + conv_b[None, :, None]
        x_act = jax.nn.silu(xconv.transpose(0, 2, 1))
        params = x_act @ W_param.T
        dt_feats = params[..., :DT_RANK]
        B_raw = params[..., DT_RANK:DT_RANK + H * N].reshape(B, Lq, H, N)
        C_raw = params[..., DT_RANK + H * N:].reshape(B, Lq, H, N)
        delta = jax.nn.softplus(dt_feats @ W_dt.T + b_dt)
        A = -jnp.exp(A_log)
        A_bar = jnp.exp(delta[..., None] * A)
        u = x_act.reshape(B, Lq, H, N)
        Bu = delta[..., None] * B_raw * u

        def step(h, inp):
            a, b, c = inp
            h = a * h + b
            return (h, c * h)
        h0 = jnp.zeros((B, H, N), x.dtype)
        _, ys = lax.scan(step, h0, (A_bar.transpose(1, 0, 2, 3), Bu.transpose(1, 0, 2, 3), C_raw.transpose(1, 0, 2, 3)))
        y = ys.transpose(1, 0, 2, 3).reshape(B, Lq, D_INNER)
        y = y + D * x_act
        y = y * jax.nn.silu(z)
        return y @ W_out.T

    def _L0_xattn_ref(q, k, attn_mask, key_padding_mask, qc_score, Wq, bq, Wk, bk):
        import jax, jax.numpy as jnp
        import numpy as np
        B, S, H = (8, 256, 64)
        qp = jnp.einsum('bsh,oh->bso', q, Wq) + bq
        kp = jnp.einsum('bth,oh->bto', k, Wk) + bk
        scaling = jnp.asarray(float(H) ** (-0.5), dtype=qp.dtype)
        scores = jnp.einsum('bsh,bth->bst', qp, kp) * scaling
        scores = scores * qc_score
        mask = attn_mask[None, :, :] | key_padding_mask[:, None, :]
        scores = jnp.where(mask, -jnp.inf, scores)
        return jax.nn.softmax(scores, axis=-1)

    def _L0_ffn_ref(x, lut, gate_idx, up_idx, down_idx):
        import jax, jax.numpy as jnp
        import numpy as np
        HIDDEN = 256
        INTER = 688
        LUT_SIZE = 16

        def _ghost_linear(x, idx, lut):
            w = lut[idx]
            return jnp.einsum('bsh,oh->bso', x, w)
        gate = _ghost_linear(x, gate_idx, lut)
        up = _ghost_linear(x, up_idx, lut)
        h = jax.nn.silu(gate) * up
        return _ghost_linear(h, down_idx, lut)
    x = _layernorm(x + _L0_attn_ref(x, L0_attn_W_in_x, L0_attn_W_in_z, L0_attn_conv_w, L0_attn_conv_b, L0_attn_W_param, L0_attn_W_dt, L0_attn_b_dt, L0_attn_A_log, L0_attn_D, L0_attn_W_out), axis=-1)
    x = _layernorm(x + _L0_xattn_ref(ctx_512, ctx_512, mask_SxS2_bk1, mask_BxS2_bf0, x, L0_xattn_Wq, L0_xattn_bq, L0_xattn_Wk, L0_xattn_bk), axis=-1)
    x = _layernorm(x + _L0_ffn_ref(x, L0_ffn_lut, L0_ffn_gate_idx, L0_ffn_up_idx, L0_ffn_down_idx), axis=-1)
    return x

_drawn_inputs = setup_inputs


def setup_inputs(seed=0):
    import zlib

    import numpy as np

    out = dict(_drawn_inputs(seed))
    spreads = {'L0_attn_D': (1.0, 0.6), 'L0_xattn_bq': (0.0, 2.0), 'L0_xattn_bk': (0.0, 2.0)}
    factors = {'ctx_512': 3.112,
     'L0_attn_W_in_x': 8.0,
     'L0_attn_W_in_z': 8.0,
     'L0_attn_conv_w': 8.0,
     'L0_attn_conv_b': 8.0,
     'L0_attn_W_param': 8.0,
     'L0_attn_W_dt': 8.0,
     'L0_attn_b_dt': 8.0,
     'L0_attn_A_log': 200.0,
     'L0_attn_W_out': 8.0,
     'L0_xattn_Wq': 2.972,
     'L0_xattn_Wk': 3.024}
    for name, (base, spread) in spreads.items():
        noise = np.random.default_rng([zlib.crc32(name.encode()), seed]).standard_normal(out[name].shape)
        drawn = base * np.exp(spread * noise) if base else spread * noise
        out[name] = jnp.asarray(drawn.astype(out[name].dtype))
    for name, factor in factors.items():
        out[name] = (out[name] * factor).astype(out[name].dtype)
    return out
```

```python
import concourse.bass as bass
from concourse import mybir
from contextlib import ExitStack


def post_norm_decoder_layer(nc: bass.Bass, x, xT, WxT, WzT, chan, WpT, WdtT, b_dt, WoT,
                            ctxT, WqT, WkT, bq, bk, attn_mask, key_mask,
                            lut, gate_idxT, up_idxT, down_idxT, out):
    f32, bf16 = mybir.dt.float32, mybir.dt.bfloat16
    i32, u8 = mybir.dt.int32, mybir.dt.uint8
    ALU, ACT = mybir.AluOpType, mybir.ActivationFunctionType

    P = 128
    T, D = x.shape
    C = WxT.shape[1]
    R, H = WdtT.shape
    N = C // H
    NB = key_mask.shape[0]
    L = T // NB
    E = ctxT.shape[0]
    I = gate_idxT.shape[1]
    V = lut.shape[0]
    K = 4
    CT, DT, IT = C // P, D // P, -(-I // P)
    IR = I - (IT - 1) * P
    NH = 2
    S = T // NH
    BH = NB // NH
    NT, TH = T // P, S // P
    LT = L // P
    Q = P // H
    SCALE = float(E) ** -0.5
    EPS = 1e-5
    MASKED = 1e38
    NPB, NQB, NMB = 3, 3, 2

    ctx = ExitStack()
    with ctx:
        def sb(name, shape, dt=f32):
            return ctx.enter_context(nc.sbuf_tensor(name, shape, dt))

        def sem(name):
            return ctx.enter_context(nc.semaphore(name))

        xT_sb = sb("xT_sb", [P, DT, T])
        x_sb = sb("x_sb", [P, NT, D])
        wx = sb("wx", [P, DT, C])
        wz = sb("wz", [P, DT, C])
        wp = sb("wp", [P, CT, R + 2 * C])
        wdt = sb("wdt", [R, H])
        wo = sb("wo", [P, CT, D])
        ch = sb("ch", [P, CT, K + 3])
        bdt = sb("bdt", [P, 1])
        ctx_sb = sb("ctx_sb", [E, T])
        wqk = sb("wqk", [E, 2, E])
        bqk = sb("bqk", [E, 2])
        am_u8 = sb("am_u8", [P, LT, L], u8)
        km_u8 = sb("km_u8", [P, NB, L], u8)
        lut_sb = sb("lut_sb", [P, V])
        GC, DC = DT * I, IT * D
        idx_in, idx_down = sb("idx_in", [P, GC], i32), sb("idx_down", [P, DC], i32)
        idx = [idx_in, idx_in, idx_down]
        idx_b = [sb(f"idx_b{w}", [P, n], bf16) for w, n in enumerate((GC, GC, DC))]
        w_ffn = [sb(f"w_ffn{w}", [P, n]) for w, n in enumerate((GC, GC, DC))]
        hit = sb("hit", [P, 2, DC], bf16)
        ident = sb("ident", [P, P])
        sel = sb("sel", [P, CT, P // N, N])
        qmask = sb("qmask", [P, Q, P])
        neg_a = sb("neg_a", [P, CT])
        qk = sb("qk", [E, 2, T])
        sc = sb("sc", [P, NT, L])
        am_big = sb("am_big", [P, LT, L])
        km_big = sb("km_big", [P, NB, L])
        mask_big = sb("mask_big", [P, NB, LT, L])
        acc = sb("acc", [P, 3, S])
        xact = sb("xact", [P, CT, T])
        zs = sb("zs", [P, CT, T])
        dtf = sb("dtf", [R, NH, S])
        sp = sb("sp", [P, 6, P])
        step = sb("step", [P, NH, S])
        abar = sb("abar", [P, 2, S])
        du = sb("du", [P, 2, S])
        hst = sb("hst", [P, 2, S])
        x1 = sb("x1", [P, NT, D])
        x2T = xT_sb
        stats = sb("stats", [P, 3 * NT, 6])
        mv = sb("mv", [P, 3 * NT, 2])
        rstd = sb("rstd", [P, 3 * NT, 2])
        mhalf = sb("mhalf", [P, 1])
        nmax = sb("nmax", [P, NT])
        psum_p = sb("psum_p", [P, NT])
        rsum = sb("rsum", [P, NT])
        no_key = sb("no_key", [P, NT])
        hf = xact[:, :, :].rearrange("p m t -> p (m t)")[:, 0:IT * S].rearrange("p (i t) -> p i t", i=IT)

        pP = [ctx.enter_context(nc.psum_tensor(f"pP{i}", [P, S], f32)) for i in range(NPB)]
        pQ = [ctx.enter_context(nc.psum_tensor(f"pQ{i}", [P, S], f32)) for i in range(NQB)]
        pM = [ctx.enter_context(nc.psum_tensor(f"pM{i}", [P, S], f32)) for i in range(NMB)]

        ld = {n: sem("ld_" + n) for n in
              ("wx", "xt0", "xt1", "ch", "wz", "dt", "wp", "ctx", "mask", "lut", "idx0", "idx1", "idx2",
               "wo", "x")}
        consts_made = sem("consts_made")
        ident_made = sem("ident_made")
        sel_made = sem("sel_made")
        qmask_made = sem("qmask_made")
        mask_made = sem("mask_made")
        idx_made = sem("idx_made")
        var_eps = sem("var_eps")
        rstd_ready = sem("rstd_ready")
        x_ready, z_ready = sem("x_ready"), sem("z_ready")
        qk_ready, score_ready = sem("qk_ready"), sem("score_ready")
        dtf_ready, dt_ready = sem("dtf_ready"), sem("dt_ready")
        delta_ready, b_ready, c_ready = sem("delta_ready"), sem("b_ready"), sem("c_ready")
        out_ready, x2T_ready = sem("out_ready"), sem("x2T_ready")
        gate_ready, up_ready, down_ready = sem("gate_ready"), sem("up_ready"), sem("down_ready")
        a_exp, a_ready = sem("a_exp"), sem("a_ready")
        tap_last, xact_ready, zs_ready = sem("tap_last"), sem("xact_ready"), sem("zs_ready")
        qk_copied, score_copied = sem("qk_copied"), sem("score_copied")
        dtf_copied, dt_biased, sp_abs, sp_exp, sp_ln = (sem(n) for n in
            ("dtf_copied", "dt_biased", "sp_abs", "sp_exp", "sp_ln"))
        abar_ready = sem("abar_ready")
        prob_ready, x2T_copied, sg_ready = sem("prob_ready"), sem("x2T_copied"), sem("sg_ready")
        taps = sem("taps")
        sp_step, step_ready = sem("sp_step"), sem("step_ready")
        du_ready, bu_ready, scanned, ch_ready, yd_ready, y_ready = (sem(n) for n in
            ("du_ready", "bu_ready", "scanned", "ch_ready", "yd_ready", "y_ready"))
        summed, stat_ready, mv_ready, normed = sem("summed"), sem("stat_ready"), sem("mv_ready"), sem("normed")
        weighed, masked, rsum_ready, attended = (sem(n) for n in
            ("weighed", "masked", "rsum_ready", "attended"))
        h_ready = sem("h_ready")
        hit_ready, w_ready = sem("hit_ready"), sem("w_ready")
        stored = sem("stored")

        block = ctx.enter_context(nc.Block())

        TAPS = K - 1

        def p_used(kind, n):
            return {"x": (taps, TAPS * (n + 1)), "z": (zs_ready, n + 1), "gate": (sg_ready, n + 1)}[kind]

        def q_used(kind, n):
            return {"delta": (du_ready, n + 1), "b": (bu_ready, n + 1), "c": (ch_ready, n + 1),
                    "up": (h_ready, n + 1)}[kind]

        def m_used(kind, n):
            return {"qk": (qk_copied, n + 1), "score": (score_copied, n + 1),
                    "dtf": (dtf_copied, n + 1), "dt": (dt_biased, n + 1),
                    "out": (summed, sum_at("out", n)), "turn": (x2T_copied, n + 1),
                    "down": (summed, sum_at("down", n))}[kind]

        SUMS = [("out", t) for t in range(NT)] + [("down", t) for t in range(NT)]

        def sum_at(kind, t):
            return SUMS.index((kind, t)) + 1

        LN = [(k, t) for h in range(NH) for k in (0, 1) for t in range(TH * h, TH * h + TH)]
        LN += [(2, t) for t in range(NT)]


        halves = [range(CT * h, CT * (h + 1)) for h in range(NH)]
        P_ORDER = [("x", u) for u in halves[0]] + [("z", u) for u in halves[0]] \
            + [("x", u) for u in halves[1]] + [("z", u) for u in halves[1]] + [("gate", n) for n in range(NH * IT)]
        Q_ORDER = [(kind, u) for u in range(NH * CT) for kind in ("b", "delta", "c")] \
            + [("up", n) for n in range(NH * IT)]
        M_ORDER = [("dtf", 0)] + [("qk", n) for n in range(4)] + [("dt", 0)] + [("score", b) for b in range(NB)] \
            + [("dtf", 1), ("dt", 1)] + [("out", t) for t in range(TH)] + [("turn", t) for t in range(TH)] \
            + [("out", t) for t in range(TH, NT)] + [("down", t) for t in range(TH)] \
            + [("turn", t) for t in range(TH, NT)] + [("down", t) for t in range(TH, NT)]

        def p_bank(kind, n):
            return pP[P_ORDER.index((kind, n)) % NPB]

        def q_bank(kind, n):
            return pQ[Q_ORDER.index((kind, n)) % NQB]

        def m_bank(kind, n):
            return pM[M_ORDER.index((kind, n)) % NMB]

        @block.sync
        def _(sp_e):
            def load(name, dst, src):
                nc.sync.dma_start(dst, src).then_inc(ld[name], 16)

            by_p = lambda a: a.rearrange("(t p) n -> p t n", p=P)
            load("wx", wx[:, :, :], by_p(WxT))
            load("xt0", xT_sb[:, :, 0:S], by_p(xT[:, 0:S]))
            load("ch", ch[:, :, :], chan.rearrange("(t p) n -> p t n", p=P))
            load("wz", wz[:, :, :], by_p(WzT))
            load("xt1", xT_sb[:, :, S:T], by_p(xT[:, S:T]))
            load("lut", lut_sb[:, :], lut.partition_broadcast(P))
            load("idx0", idx[0][:, :].rearrange("p (t n) -> p t n", t=DT), by_p(gate_idxT))
            load("dt", wdt[:, :], WdtT)
            for q in range(Q):
                load("dt", bdt[q * H:(q + 1) * H, :], b_dt)
            for t in range(CT):
                load("wp", wp[:, t, :], WpT[t * P:(t + 1) * P, :])
            load("ctx", ctx_sb[:, :], ctxT)
            load("ctx", wqk[:, 0, :], WqT)
            load("ctx", wqk[:, 1, :], WkT)
            load("ctx", bqk[:, 0:1], bq)
            load("ctx", bqk[:, 1:2], bk)
            sp_e.wait_ge(idx_made, 1)
            load("idx1", idx[1][:, :].rearrange("p (t n) -> p t n", t=DT), by_p(up_idxT))
            load("wo", wo[:, :, :], by_p(WoT))
            load("x", x_sb[:, :, :], by_p(x))
            load("mask", am_u8[:, :, :], by_p(attn_mask))
            load("mask", km_u8[:, :, :], key_mask.partition_broadcast(P))
            full = (IT - 1) * P
            load("idx2", idx[2][:, 0:(IT - 1) * D].rearrange("p (t n) -> p t n", n=D), by_p(down_idxT[0:full, :]))
            load("idx2", idx[2][0:IR, (IT - 1) * D:DC], down_idxT[full:I, :])
            for t in range(NT):
                sp_e.wait_ge(normed, 2 * NT + t + 1)
                nc.sync.dma_start(out[t * P:(t + 1) * P, :], x1[:, t, :]).then_inc(stored, 16)
            sp_e.wait_ge(stored, 16 * NT)

        @block.gpsimd
        def _(pool):
            nc.gpsimd.memset(ident[:, :], 0.0).then_inc(consts_made, 1)
            nc.gpsimd.memset(sel[:, :, :, :], 0.0).then_inc(consts_made, 1)
            nc.gpsimd.memset(qmask[:, :, :], 1.0).then_inc(consts_made, 1)
            nc.gpsimd.memset(mhalf[:, :], -0.5).then_inc(consts_made, 1)
            nc.gpsimd.memset(idx[2][:, (IT - 1) * D:DC].bitcast(f32), 0.0).then_inc(consts_made, 1)
            pool.wait_ge(consts_made, 5)
            nc.gpsimd.affine_select(out=ident[:, :], in_=ident[:, :], compare_op=ALU.not_equal, fill=1.0,
                                    base=0, pattern=[[-1, P]], channel_multiplier=1).then_inc(ident_made, 1)
            for q in range(Q):
                pool.wait_ge(sel_made, q) if q else pool.wait_ge(ident_made, 1)
                rows = sel[q * H:(q + 1) * H, :, :, :].rearrange("p t g n -> p (t g) n")
                nc.gpsimd.affine_select(out=rows, in_=rows, compare_op=ALU.not_equal, fill=1.0, base=0,
                                        pattern=[[-1, H], [0, N]], channel_multiplier=1).then_inc(sel_made, 1)
            pool.wait_ge(sel_made, Q)
            nc.gpsimd.affine_select(out=qmask[:, :, :], in_=qmask[:, :, :], compare_op=ALU.is_ge, fill=0.0,
                                    base=0, pattern=[[-H, Q], [0, P]], channel_multiplier=1).then_inc(qmask_made, 1)
            pool.wait_ge(qmask_made, 1)
            nc.gpsimd.affine_select(out=qmask[:, :, :], in_=qmask[:, :, :], compare_op=ALU.is_ge, fill=0.0,
                                    base=H - 1, pattern=[[H, Q], [0, P]], channel_multiplier=-1)\
                .then_inc(qmask_made, 1)
            for w in range(3):
                pool.wait_ge(ld[f"idx{w}"], 16 if w < 2 else 32)
                nc.gpsimd.tensor_copy(idx_b[w][:, :], idx[w][:, :]).then_inc(idx_made, 1)
            pool.wait_ge(ld["mask"], 32)
            nc.gpsimd.tensor_scalar(am_big[:, :, :], am_u8[:, :, :], MASKED, None, ALU.mult)\
                .then_inc(mask_made, 1)
            nc.gpsimd.tensor_scalar(km_big[:, :, :], km_u8[:, :, :], MASKED, None, ALU.mult)\
                .then_inc(mask_made, 1)
            pool.wait_ge(mask_made, 2)
            for b in range(NB):
                nc.gpsimd.tensor_tensor(mask_big[:, b, :, :], am_big[:, :, :],
                                        km_big[:, b:b + 1, :].to_broadcast([P, LT, L]),
                                        ALU.add).then_inc(mask_made, 1)
            for n in range(len(LN)):
                pool.wait_ge(mv_ready, n + 1)
                nc.gpsimd.tensor_scalar(rstd[:, n, 0:1], mv[:, n, 1:2], EPS, None, ALU.add).then_inc(var_eps, 1)
                pool.wait_ge(var_eps, n + 1)
                nc.gpsimd.tensor_tensor(rstd[:, n, 1:2], rstd[:, n, 0:1], mhalf[:, :], ALU.pow)\
                    .then_inc(rstd_ready, 1)

        @block.tensor
        def _(pe):
            rings = {"P": (pP, P_ORDER, p_used), "Q": (pQ, Q_ORDER, q_used), "M": (pM, M_ORDER, m_used)}

            def bank(r, kind, n):
                banks, order, used = rings[r]
                at, size = order.index((kind, n)), len(banks)
                if at >= size:
                    pe.wait_ge(*used(*order[at - size]))
                return banks[at % size]

            def product(dst, pairs):
                for k, (lhsT, rhs) in enumerate(pairs):
                    last = nc.tensor.matmul(dst, lhsT, rhs, start=(k == 0), stop=(k == len(pairs) - 1))
                return last

            def project(kind, w, ready, h, m):
                dst = bank("P", kind, CT * h + m)
                product(dst[:, :], [(w[:, k, m * P:(m + 1) * P], xT_sb[:, k, h * S:(h + 1) * S])
                                    for k in range(DT)]).then_inc(ready, 1)

            def step_size(h):
                pe.wait_ge(xact_ready, CT * (h + 1))
                dst = bank("M", "dtf", h)
                product(dst[:, :], [(wp[:, k, 0:R], xact[:, k, h * S:(h + 1) * S]) for k in range(CT)])\
                    .then_inc(dtf_ready, 1)

            def step_heads(h):
                dst = bank("M", "dt", h)
                pe.wait_ge(dtf_copied, h + 1)
                for q in range(Q):
                    last = nc.tensor.matmul(dst[q * H:(q + 1) * H, 0:P], wdt[:, :], dtf[:, h, q * P:(q + 1) * P],
                                            start=True, stop=True)
                last.then_inc(dt_ready, 1)

            def states(h, m):
                u = CT * h + m
                cols = slice(h * S, (h + 1) * S)
                dst = bank("Q", "b", u)
                product(dst[:, :], [(wp[:, k, R + m * P:R + (m + 1) * P], xact[:, k, cols]) for k in range(CT)])\
                    .then_inc(b_ready, 1)
                dst = bank("Q", "delta", u)
                if m == 0:
                    pe.wait_ge(step_ready, h + 1)
                product(dst[:, :], [(sel[:, m, :, :], step[:, h, :])]).then_inc(delta_ready, 1)
                dst = bank("Q", "c", u)
                product(dst[:, :], [(wp[:, k, R + C + m * P:R + C + (m + 1) * P], xact[:, k, cols])
                                    for k in range(CT)]).then_inc(c_ready, 1)

            def mix_out(t):
                dst = bank("M", "out", t)
                pe.wait_ge(y_ready, CT * (t // TH + 1))
                product(dst[:, 0:D], [(zs[:, k, t * P:(t + 1) * P], wo[:, k, :]) for k in range(CT)])\
                    .then_inc(out_ready, 1)

            def turn(t):
                dst = bank("M", "turn", t)
                pe.wait_ge(normed, LN.index((1, t)) + 1)
                for k in range(DT):
                    last = nc.tensor.transpose(dst[:, k * P:(k + 1) * P], x1[:, t, k * P:(k + 1) * P], ident[:, :])
                last.then_inc(x2T_ready, 1)

            def ffn_in(h, i):
                n, M = IT * h + i, (P if i < IT - 1 else IR)
                if i == 0:
                    pe.wait_ge(x2T_copied, TH * (h + 1))
                    if h == 0:
                        pe.wait_ge(w_ready, 2 * V)
                for r, kind, w, ready in (("P", "gate", w_ffn[0], gate_ready), ("Q", "up", w_ffn[1], up_ready)):
                    dst = bank(r, kind, n)
                    product(dst[0:M, :], [(w[:, k * I + i * P:k * I + i * P + M], x2T[:, k, h * S:(h + 1) * S])
                                          for k in range(DT)]).then_inc(ready, 1)

            def ffn_out(t):
                dst = bank("M", "down", t)
                h, o = t // TH, (t % TH) * P
                if t == 0:
                    pe.wait_ge(w_ready, 3 * V)
                pe.wait_ge(h_ready, IT * (h + 1))
                rows = [P] * (IT - 1) + [IR]
                product(dst[:, 0:D], [(hf[0:rows[i], i, o:o + P], w_ffn[2][0:rows[i], i * D:(i + 1) * D])
                                      for i in range(IT)]).then_inc(down_ready, 1)

            pe.wait_ge(ld["wx"], 16)
            pe.wait_ge(ld["xt0"], 16)
            for m in range(CT):
                project("x", wx, x_ready, 0, m)
            pe.wait_ge(ld["wz"], 16)
            for m in range(CT):
                project("z", wz, z_ready, 0, m)
            pe.wait_ge(ld["xt1"], 16)
            for m in range(CT):
                project("x", wx, x_ready, 1, m)
            for m in range(CT):
                project("z", wz, z_ready, 1, m)
            pe.wait_ge(ld["wp"], 16 * CT)
            step_size(0)
            pe.wait_ge(ld["ctx"], 16 * 5)
            for n in range(4):
                dst = bank("M", "qk", n)
                product(dst[0:E, :], [(wqk[:, n // 2, :], ctx_sb[:, (n % 2) * S:(n % 2 + 1) * S])])\
                    .then_inc(qk_ready, 1)
            pe.wait_ge(ld["dt"], 16 * (1 + Q))
            step_heads(0)
            pe.wait_ge(qk_copied, 4)
            for b in range(NB):
                dst = bank("M", "score", b)
                for s in range(LT):
                    o = b * L + s * P
                    last = nc.tensor.matmul(dst[:, s * L:(s + 1) * L], qk[:, 0, o:o + P],
                                            qk[:, 1, b * L:(b + 1) * L], start=True, stop=True)
                last.then_inc(score_ready, 1)
            pe.wait_ge(sel_made, Q)
            for m in range(CT):
                states(0, m)
            step_size(1)
            step_heads(1)
            pe.wait_ge(ld["wo"], 16)
            for m in range(CT):
                states(1, m)
                mix_out(m)
            pe.wait_ge(ident_made, 1)
            for t in range(TH):
                turn(t)
            ffn_in(0, 0)
            for t in range(TH, NT):
                mix_out(t)
            for i in range(1, IT):
                ffn_in(0, i)
            for t in range(TH):
                ffn_out(t)
            for t in range(TH, NT):
                turn(t)
            for i in range(IT):
                ffn_in(1, i)
            for t in range(TH, NT):
                ffn_out(t)

        @block.scalar
        def _(act):
            ALOG = K + 2

            def conv_first(u):
                act.wait_ge(x_ready, u + 1)
                if u >= 3:
                    act.wait_ge(xact_ready, u - 2)
                m = u % CT
                nc.scalar.activation(acc[:, u % 3, :], p_bank("x", u)[:, :], ACT.Identity,
                                     bias=ch[:, m, K:K + 1], scale=ch[:, m, K - 1:K]).then_inc(tap_last, 1)

            def conv_silu(u):
                act.wait_ge(taps, TAPS * (u + 1))
                nc.scalar.activation(xact[:, u % CT, (u // CT) * S:(u // CT + 1) * S], acc[:, u % 3, :],
                                     ACT.Silu).then_inc(xact_ready, 1)

            def z_silu(u):
                act.wait_ge(z_ready, u + 1)
                nc.scalar.activation(zs[:, u % CT, (u // CT) * S:(u // CT + 1) * S], p_bank("z", u)[:, :],
                                     ACT.Silu).then_inc(zs_ready, 1)

            def dtf_copy(h):
                act.wait_ge(dtf_ready, h + 1)
                nc.scalar.activation(dtf[:, h, :], m_bank("dtf", h)[:, :], ACT.Copy).then_inc(dtf_copied, 1)

            def softplus_parts(h):
                act.wait_ge(dt_ready, h + 1)
                if h:
                    act.wait_ge(step_ready, h)
                nc.scalar.activation(sp[:, 0, :], m_bank("dt", h)[:, 0:P], ACT.Identity, bias=bdt[:, 0:1])\
                    .then_inc(dt_biased, 1)
                act.wait_ge(dt_biased, h + 1)
                nc.scalar.activation(sp[:, 1, :], sp[:, 0, :], ACT.Abs).then_inc(sp_abs, 1)
                act.wait_ge(sp_abs, h + 1)
                nc.scalar.activation(sp[:, 2, :], sp[:, 1, :], ACT.Exp, scale=-1.0).then_inc(sp_exp, 1)
                act.wait_ge(sp_exp, h + 1)
                nc.scalar.activation(sp[:, 3, :], sp[:, 2, :], ACT.Ln, bias=1.0).then_inc(sp_ln, 1)

            def decay(u):
                act.wait_ge(delta_ready, u + 1)
                if u >= 2:
                    act.wait_ge(scanned, BH * (u - 1))
                nc.scalar.activation(abar[:, u % 2, :], q_bank("delta", u)[:, :], ACT.Exp,
                                     scale=neg_a[:, u % CT:u % CT + 1]).then_inc(abar_ready, 1)

            def prob(t):
                act.wait_ge(masked, t + 1)
                nc.scalar.activation(sc[:, t, :], sc[:, t, :], ACT.Exp, bias=nmax[:, t:t + 1], scale=-1.0,
                                     accum_out=psum_p[:, t:t + 1]).then_inc(prob_ready, 1)

            def turn_copy(t):
                act.wait_ge(x2T_ready, t + 1)
                nc.scalar.activation(x2T[:, :, t * P:(t + 1) * P],
                                     m_bank("turn", t)[:, 0:DT * P].rearrange("p (k n) -> p k n", k=DT),
                                     ACT.Copy).then_inc(x2T_copied, 1)

            def gate_silu(n):
                i, M = n % IT, (P if n % IT < IT - 1 else IR)
                act.wait_ge(gate_ready, n + 1)
                if n == IT:
                    act.wait_ge(down_ready, TH)
                nc.scalar.activation(hf[0:M, i, :], p_bank("gate", n)[0:M, :], ACT.Silu).then_inc(sg_ready, 1)

            act.wait_ge(ld["ch"], 16)
            for h in range(NH):
                for u in halves[h]:
                    conv_first(u)
                    if u > CT * h:
                        conv_silu(u - 1)
                z_silu(CT * h)
                conv_silu(CT * h + CT - 1)
                for u in halves[h][1:]:
                    z_silu(u)
            nc.scalar.preload_act_table_set("natural_log_exp_and_others")
            nc.scalar.activation(neg_a[:, :], ch[:, :, ALOG], ACT.Exp).then_inc(a_exp, 1)
            act.wait_ge(a_exp, 1)
            nc.scalar.mul(neg_a[:, :], neg_a[:, :], -1.0).then_inc(a_ready, 1)
            dtf_copy(0)
            act.wait_ge(ld["ctx"], 16 * 5)
            for n in range(4):
                act.wait_ge(qk_ready, n + 1)
                nc.scalar.activation(qk[:, n // 2, (n % 2) * S:(n % 2 + 1) * S], m_bank("qk", n)[0:E, :],
                                     ACT.Identity, bias=bqk[:, n // 2:n // 2 + 1]).then_inc(qk_copied, 1)
            act.wait_ge(ld["dt"], 16 * (1 + Q))
            softplus_parts(0)
            for b in range(NB):
                act.wait_ge(score_ready, b + 1)
                nc.scalar.activation(sc[:, LT * b:LT * (b + 1), :],
                                     m_bank("score", b)[:, :].rearrange("p (s l) -> p s l", s=LT),
                                     ACT.Copy, scale=-SCALE).then_inc(score_copied, 1)
            act.wait_ge(a_ready, 1)
            for m in range(CT):
                decay(m)
            dtf_copy(1)
            softplus_parts(1)
            for m in range(CT):
                decay(CT + m)
            for t in range(TH):
                prob(t)
            for t in range(TH):
                turn_copy(t)
            gate_silu(0)
            for t in range(TH, NT):
                prob(t)
            for n in range(1, IT):
                gate_silu(n)
            for t in range(TH, NT):
                turn_copy(t)
            for n in range(IT, NH * IT):
                gate_silu(n)

        @block.vector
        def _(dve):
            def conv_taps(u):
                m = u % CT
                a = acc[:, u % 3, :].rearrange("p (b l) -> p b l", b=BH)
                src = p_bank("x", u)[:, :].rearrange("p (b l) -> p b l", b=BH)
                dve.wait_ge(tap_last, u + 1)
                for k in range(TAPS):
                    back = K - 1 - k
                    if k:
                        dve.wait_ge(taps, TAPS * u + k)
                    nc.vector.scalar_tensor_tensor(out=a[:, :, back:L], in0=src[:, :, 0:L - back],
                                                   scalar=ch[:, m, k:k + 1], in1=a[:, :, back:L],
                                                   op0=ALU.mult, op1=ALU.add).then_inc(taps, 1)

            def softplus(h):
                base = 4 * h
                dve.wait_ge(sp_exp, h + 1)
                nc.vector.tensor_scalar(sp[:, 4, :], sp[:, 2, :], 1.0, -1.0, ALU.add, ALU.add).then_inc(sp_step, 1)
                dve.wait_ge(sp_step, base + 1)
                nc.vector.tensor_tensor(sp[:, 4, :], sp[:, 2, :], sp[:, 4, :], ALU.subtract).then_inc(sp_step, 1)
                dve.wait_ge(sp_step, base + 2)
                dve.wait_ge(sp_ln, h + 1)
                nc.vector.tensor_tensor(sp[:, 4, :], sp[:, 4, :], sp[:, 3, :], ALU.add).then_inc(sp_step, 1)
                dve.wait_ge(sp_step, base + 3)
                nc.vector.scalar_tensor_tensor(out=sp[:, 5, :], in0=sp[:, 0, :], scalar=0.0, in1=sp[:, 4, :],
                                               op0=ALU.max, op1=ALU.add).then_inc(sp_step, 1)
                dve.wait_ge(sp_step, base + 4)
                dve.wait_ge(qmask_made, 2)
                nc.vector.tensor_tensor(step[:, h, :].rearrange("p (q n) -> p q n", q=Q), qmask[:, :, :],
                                        sp[:, 5:6, :].to_broadcast([P, Q, P]), ALU.mult).then_inc(step_ready, 1)

            def state_space(u):
                m, h, s = u % CT, u // CT, u % 2
                cols = slice(h * S, (h + 1) * S)
                dve.wait_ge(delta_ready, u + 1)
                dve.wait_ge(abar_ready, u + 1)
                nc.vector.tensor_tensor(du[:, s, :], q_bank("delta", u)[:, :], xact[:, m, cols], ALU.mult)\
                    .then_inc(du_ready, 1)
                dve.wait_ge(du_ready, u + 1)
                dve.wait_ge(b_ready, u + 1)
                nc.vector.tensor_tensor(du[:, s, :], q_bank("b", u)[:, :], du[:, s, :], ALU.mult)\
                    .then_inc(bu_ready, 1)
                dve.wait_ge(bu_ready, u + 1)
                for b in range(BH):
                    c = slice(b * L, (b + 1) * L)
                    nc.vector.tensor_tensor_scan(hst[:, s, c], abar[:, s, c], du[:, s, c], 0.0,
                                                 ALU.mult, ALU.add).then_inc(scanned, 1)
                dve.wait_ge(scanned, BH * (u + 1))
                dve.wait_ge(c_ready, u + 1)
                nc.vector.tensor_tensor(hst[:, s, :], q_bank("c", u)[:, :], hst[:, s, :], ALU.mult)\
                    .then_inc(ch_ready, 1)
                dve.wait_ge(ch_ready, u + 1)
                nc.vector.scalar_tensor_tensor(out=hst[:, s, :], in0=xact[:, m, cols], scalar=ch[:, m, K + 1:K + 2],
                                               in1=hst[:, s, :], op0=ALU.mult, op1=ALU.add).then_inc(yd_ready, 1)
                dve.wait_ge(yd_ready, u + 1)
                dve.wait_ge(zs_ready, u + 1)
                nc.vector.tensor_tensor(zs[:, m, cols], zs[:, m, cols], hst[:, s, :], ALU.mult)\
                    .then_inc(y_ready, 1)

            def norm_stats(n, src):
                nc.vector.bn_stats(stats[:, n, :], src).then_inc(stat_ready, 1)
                dve.wait_ge(stat_ready, n + 1)
                nc.vector.bn_aggr(mv[:, n, :], stats[:, n, :]).then_inc(mv_ready, 1)

            def normalize(n, dst, src):
                dve.wait_ge(rstd_ready, n + 1)
                nc.vector.tensor_scalar(dst, src, mv[:, n, 0:1], rstd[:, n, 1:2], ALU.subtract, ALU.mult)\
                    .then_inc(normed, 1)

            def mixed(t):
                dve.wait_ge(out_ready, t + 1)
                nc.vector.tensor_tensor(x_sb[:, t, :], m_bank("out", t)[:, 0:D], x_sb[:, t, :], ALU.add)\
                    .then_inc(summed, 1)
                dve.wait_ge(summed, sum_at("out", t))
                norm_stats(LN.index((0, t)), x_sb[:, t, :])

            def weigh(t):
                n = LN.index((0, t))
                normalize(n, x1[:, t, :], x_sb[:, t, :])
                dve.wait_ge(normed, n + 1)
                nc.vector.tensor_tensor(sc[:, t, :], sc[:, t, :], x1[:, t, :], ALU.mult).then_inc(weighed, 1)
                dve.wait_ge(weighed, t + 1)
                nc.vector.tensor_tensor_reduce(out=sc[:, t, :], in0=sc[:, t, :], in1=mask_big[:, t // LT, t % LT, :],
                                               scale=1.0, scalar=3e38, op0=ALU.add, op1=ALU.min,
                                               accum_out=nmax[:, t:t + 1]).then_inc(masked, 1)

            def attend(t):
                dve.wait_ge(prob_ready, t + 1)
                nc.vector.reciprocal(rsum[:, t:t + 1], psum_p[:, t:t + 1]).then_inc(rsum_ready, 1)
                nc.vector.tensor_scalar(no_key[:, t:t + 1], nmax[:, t:t + 1], MASKED / 2, MASKED, ALU.is_ge,
                                        ALU.mult).then_inc(rsum_ready, 1)
                dve.wait_ge(rsum_ready, 3 * t + 2)
                nc.vector.scalar_tensor_tensor(out=rsum[:, t:t + 1], in0=no_key[:, t:t + 1], scalar=MASKED,
                                               in1=rsum[:, t:t + 1], op0=ALU.mult, op1=ALU.add)\
                    .then_inc(rsum_ready, 1)
                dve.wait_ge(rsum_ready, 3 * t + 3)
                nc.vector.scalar_tensor_tensor(out=sc[:, t, :], in0=sc[:, t, :], scalar=rsum[:, t:t + 1],
                                               in1=x1[:, t, :], op0=ALU.mult, op1=ALU.add).then_inc(attended, 1)
                dve.wait_ge(attended, t + 1)
                norm_stats(LN.index((1, t)), sc[:, t, :])

            def norm2(t):
                normalize(LN.index((1, t)), x1[:, t, :], sc[:, t, :])

            def hidden(n):
                i, M = n % IT, (P if n % IT < IT - 1 else IR)
                dve.wait_ge(sg_ready, n + 1)
                dve.wait_ge(up_ready, n + 1)
                nc.vector.tensor_tensor(hf[0:M, i, :], q_bank("up", n)[0:M, :], hf[0:M, i, :], ALU.mult)\
                    .then_inc(h_ready, 1)

            def ffn_sum(t):
                dve.wait_ge(down_ready, t + 1)
                nc.vector.tensor_tensor(x1[:, t, :], m_bank("down", t)[:, 0:D], x1[:, t, :], ALU.add)\
                    .then_inc(summed, 1)
                dve.wait_ge(summed, sum_at("down", t))
                norm_stats(LN.index((2, t)), x1[:, t, :])

            def norm3(t):
                normalize(LN.index((2, t)), x1[:, t, :], x1[:, t, :])

            def decode(w, v0, v1):
                n = w_ffn[w].shape[1]
                for v in range(v0, v1):
                    g = w * V + v
                    if v == 0:
                        dve.wait_ge(idx_made, w + 1)
                        dve.wait_ge(ld["lut"], 16)
                        nc.vector.tensor_scalar(w_ffn[w][:, :], idx_b[w][:, :], float(v), lut_sb[:, v:v + 1],
                                                ALU.is_equal, ALU.mult).then_inc(w_ready, 1)
                        continue
                    nc.vector.tensor_scalar(hit[:, v % 2, 0:n], idx_b[w][:, :], float(v), None,
                                            ALU.is_equal).then_inc(hit_ready, 1)
                    dve.wait_ge(hit_ready, w * (V - 1) + v)
                    dve.wait_ge(w_ready, g)
                    nc.vector.scalar_tensor_tensor(out=w_ffn[w][:, :], in0=hit[:, v % 2, 0:n],
                                                   scalar=lut_sb[:, v:v + 1], in1=w_ffn[w][:, :],
                                                   op0=ALU.mult, op1=ALU.add).then_inc(w_ready, 1)

            dve.wait_ge(ld["ch"], 16)
            for u in range(NH * CT):
                conv_taps(u)
            softplus(0)
            for m in range(CT):
                state_space(m)
                decode(0, 4 * m, 4 * m + 4)
            softplus(1)
            dve.wait_ge(ld["x"], 16)
            for m in range(CT):
                state_space(CT + m)
                mixed(m)
                decode(1, 4 * m, 4 * m + 4)
            dve.wait_ge(mask_made, 2 + NB)
            for t in range(TH):
                weigh(t)
            for t in range(TH):
                attend(t)
            for t in range(TH):
                norm2(t)
            hidden(0)
            for t in range(TH, NT):
                mixed(t)
            for t in range(TH, NT):
                weigh(t)
            for t in range(TH, NT):
                attend(t)
            for t in range(TH, NT):
                norm2(t)
            decode(2, 0, V)
            for n in range(1, IT):
                hidden(n)
            for t in range(TH):
                ffn_sum(t)
            for t in range(TH):
                norm3(t)
            for n in range(IT, NH * IT):
                hidden(n)
            for t in range(TH, NT):
                ffn_sum(t)
            for t in range(TH, NT):
                norm3(t)


def kernel(**inputs):
    import numpy as np
    import concourse.bacc as bacc
    from concourse import mybir as mb
    from concourse.bass_utils import run_bass_kernel_spmd

    a = {n: np.asarray(v) for n, v in inputs.items()}
    B, L, D = a["x"].shape
    flat = a["x"].reshape(B * L, D)
    pre = "L0_attn_"
    C = a[pre + "W_in_x"].shape[0]
    col = lambda n: a[n].reshape(-1, 1)
    device = {
        "x": flat, "xT": flat.T,
        "WxT": a[pre + "W_in_x"].T, "WzT": a[pre + "W_in_z"].T,
        "chan": np.concatenate([a[pre + "conv_w"].reshape(C, -1), col(pre + "conv_b"), col(pre + "D"),
                                col(pre + "A_log")], axis=1),
        "WpT": a[pre + "W_param"].T, "WdtT": a[pre + "W_dt"].T, "b_dt": col(pre + "b_dt"),
        "WoT": a[pre + "W_out"].T,
        "ctxT": a["ctx_512"].reshape(B * L, -1).T,
        "WqT": a["L0_xattn_Wq"].T, "WkT": a["L0_xattn_Wk"].T,
        "bq": col("L0_xattn_bq"), "bk": col("L0_xattn_bk"),
        "attn_mask": a["mask_SxS2_bk1"], "key_mask": a["mask_BxS2_bf0"],
        "lut": a["L0_ffn_lut"], "gate_idxT": a["L0_ffn_gate_idx"].T, "up_idxT": a["L0_ffn_up_idx"].T,
        "down_idxT": a["L0_ffn_down_idx"].T,
    }
    nc = bacc.Bacc("TRN2", target_bir_lowering=False, num_devices=1)
    arrays, args = {}, []
    for name, v in device.items():
        v = np.ascontiguousarray(v)
        arrays[f"in_{name}"] = v
        args.append(nc.dram_tensor(f"in_{name}", v.shape, mb.dt.from_np(v.dtype), kind="ExternalInput").ap())
    args.append(nc.dram_tensor("out_y", (B * L, D), mb.dt.float32, kind="ExternalOutput").ap())
    post_norm_decoder_layer(nc, *args)
    r = run_bass_kernel_spmd(nc, [arrays], core_ids=[0])
    return r.results[0]["out_y"].reshape(B, L, D)
```

```python
import concourse.bass as bass
from concourse import mybir
from contextlib import ExitStack


def post_norm_decoder_layer(nc: bass.Bass, x, xT, WxT, WzT, chan, WpT, WdtT, b_dt, WoT,
                            ctxT, WqT, WkT, bq, bk, attn_mask, key_mask,
                            lut, gate_idxT, up_idxT, down_idxT, out):
    f32, bf16, f32r = mybir.dt.float32, mybir.dt.bfloat16, mybir.dt.float32r
    i32, u8 = mybir.dt.int32, mybir.dt.uint8
    ALU, ACT = mybir.AluOpType, mybir.ActivationFunctionType

    P = 128
    T, D = x.shape
    C = WxT.shape[1]
    R, H = WdtT.shape
    N = C // H
    NB = key_mask.shape[0]
    L = T // NB
    E = ctxT.shape[0]
    I = gate_idxT.shape[1]
    V = lut.shape[0]
    K = 4
    CT, DT, IT = C // P, D // P, -(-I // P)
    IR = I - (IT - 1) * P
    IP = IT * P
    NH = 2
    S = T // NH
    BH = NB // NH
    NT, TH = T // P, S // P
    LT = L // P
    Q = P // H
    SCALE = float(E) ** -0.5
    EPS = 1e-5
    MASKED = 1e38
    NPB, NQB, NMB = 3, 3, 2

    ctx = ExitStack()
    with ctx:
        G = 32
        J = V // (P // G)
        IC = I // 2
        CHUNKS = [(w, k, c, IC) for w in (0, 1) for k in range(DT) for c in (0, IC)] \
            + [(2, i, 0, D) for i in range(IT)]
        CH = (P // G) * IC
        NCH_IN = 2 * DT * 2

        def sb(name, shape, dt=f32):
            return ctx.enter_context(nc.sbuf_tensor(name, shape, dt))

        def sem(name):
            return ctx.enter_context(nc.semaphore(name))

        WPC = R + 2 * C
        early = sb("early", [P, max(DT * T + 2 * DT * C + 2 * WPC, (J + 2) * CH // 2 + 2 * CH)])
        xT_sb = early[:, 0:DT * T].rearrange("p (k t) -> p k t", k=DT)
        wx, wz = (early[:, at:at + DT * C].rearrange("p (k c) -> p k c", k=DT)
                  for at in (DT * T, DT * T + DT * C))
        wp_in = early[:, DT * T + 2 * DT * C:DT * T + 2 * DT * C + 2 * WPC].rearrange("p (s c) -> p s c", s=2)
        hit = early[:, 0:J * CH // 2].bitcast(bf16).rearrange("p (j n) -> p j n", j=J)
        idx_rel = early[:, J * CH // 2:(J + 2) * CH // 2].bitcast(bf16).rearrange("p (s n) -> p s n", s=2)
        idx_in = early[:, (J + 2) * CH // 2:(J + 2) * CH // 2 + 2 * CH].bitcast(i32)\
            .rearrange("p (s n) -> p s n", s=2)
        x_sb = sb("x_sb", [P, NT, D])
        wdt = sb("wdt", [R, H])
        wo = sb("wo", [P, CT, D])
        ch = sb("ch", [P, CT, K + 3])
        bdt = sb("bdt", [P, 1])
        du = sb("du", [P, 2, S])
        ctx_sb = du[0:E, :, :].rearrange("p s n -> p (s n)")
        wqk = sb("wqk", [E, 2, E])
        bqk = sb("bqk", [E, 2])
        am_u8 = sb("am_u8", [P, LT, L], u8)
        km_u8 = sb("km_u8", [P, NB, L], u8)
        lut_in = sb("lut_in", [P, J])
        wp_hi, wp_lo = (sb(n, [P, CT, R + 2 * C], f32r) for n in ("wp_hi", "wp_lo"))
        w_in = [sb(n, [P, 2, DT, IP], f32r) for n in ("w_in_hi", "w_in_lo")]
        w_down = [a[:, :, :].rearrange("p k n -> p (k n)")[:, 0:IT * D].rearrange("p (i n) -> p i n", i=IT)
                  for a in (wp_hi, wp_lo)]

        def weights(c):
            w, k, c0, n = CHUNKS[c]
            return [a[:, k, :] for a in w_down] if w == 2 else [a[:, w, k, c0:c0 + n] for a in w_in]

        first_entry = sb("first_entry", [P, 1])
        eye = sb("eye", [P, G], bf16)
        lut_rest = sb("lut_rest", [P, 2, J])
        lut_part = sb("lut_part", [P, 3, J], bf16)
        lut_diag = sb("lut_diag", [P, 3, J, G], bf16)
        ident = sb("ident", [P, P])
        dtf = sb("dtf", [R, S])
        sel = dtf[:, :].rearrange("p (t g n) -> p t g n", t=CT, n=N)
        sel_r = sb("sel_r", [P, C], f32r)
        qmask = sb("qmask", [P, Q, P], bf16)
        neg_a = sb("neg_a", [P, CT])
        qk = x_sb[0:E, :, :].rearrange("p (a t) d -> p a (t d)", a=2)
        sc = sb("sc", [P, NT, L])
        abar = sb("abar", [P, 2, S])
        big = abar[:, :, :].rearrange("p s n -> p (s n)").bitcast(bf16)
        am_big = big[:, 0:LT * L].rearrange("p (s l) -> p s l", s=LT)
        km_big = big[:, LT * L:(LT + NB) * L].rearrange("p (b l) -> p b l", b=NB)
        mask_big = sb("mask_big", [P, NB, LT, L], bf16)
        acc = sb("acc", [P, 3, S])
        xact = sb("xact", [P, CT, T])
        xact_hi, xact_lo = (sb(n, [P, CT * T], f32r) for n in ("xact_hi", "xact_lo"))
        zs = sb("zs", [P, CT, T])
        sp = sb("sp", [P, 5, P])
        sp_hi = sb("sp_hi", [P, P], f32r)
        step_hi, step_lo = (sb(n, [P, S], f32r) for n in ("step_hi", "step_lo"))
        hst = du
        x1 = x_sb
        stats = sb("stats", [P, 3 * NT, 6])
        mv = sb("mv", [P, 3 * NT, 2])
        rstd = sb("rstd", [P, 3 * NT, 3])
        mhalf = sb("mhalf", [P, 1])
        nmax = sb("nmax", [P, NT])
        psum_p = sb("psum_p", [P, NT])
        rsum = sb("rsum", [P, NT])
        guard = sb("guard", [P, NT, 3])
        hf_hi, hf_lo = (a[:, 0:IT * S].rearrange("p (i t) -> p i t", i=IT) for a in (xact_hi, xact_lo))
        x2T_hi, x2T_lo = (a[:, IT * S:IT * S + DT * S].rearrange("p (k t) -> p k t", k=DT)
                          for a in (xact_hi, xact_lo))

        def value(a):
            return a.bitcast(f32)

        pP = [ctx.enter_context(nc.psum_tensor(f"pP{i}", [P, S], f32)) for i in range(NPB)]
        pQ = [ctx.enter_context(nc.psum_tensor(f"pQ{i}", [P, S], f32)) for i in range(NQB)]
        pM = [ctx.enter_context(nc.psum_tensor(f"pM{i}", [P, S], f32)) for i in range(NMB)]

        ld = {n: sem("ld_" + n) for n in
              ("wx0", "wx1", "xt0", "xt1", "ch", "wz", "dt", "wp0", "wp1", "ctx", "mask", "lut", "idx0", "idx1",
               "wo", "x")}
        consts_made = sem("consts_made")
        ident_made = sem("ident_made")
        sel_made = sem("sel_made")
        qmask_made, pad_made = sem("qmask_made"), sem("pad_made")
        mask_made = sem("mask_made")
        eye_made, lut_step, lut_made = sem("eye_made"), sem("lut_step"), sem("lut_made")
        wp_lo_ready, xact_lo_ready = sem("wp_lo_ready"), sem("xact_lo_ready")
        idx_cleared = sem("idx_cleared")
        var_eps = sem("var_eps")
        rstd_made, rstd_ready = sem("rstd_made"), sem("rstd_ready")
        guard_step, guarded = sem("guard_step"), sem("guarded")
        x_ready, z_ready = sem("x_ready"), sem("z_ready")
        qk_ready, score_ready = sem("qk_ready"), sem("score_ready")
        dtf_ready, dt_ready = sem("dtf_ready"), sem("dt_ready")
        delta_ready, b_ready, c_ready = sem("delta_ready"), sem("b_ready"), sem("c_ready")
        out_ready, x2T_ready = sem("out_ready"), sem("x2T_ready")
        gate_ready, up_ready, down_ready = sem("gate_ready"), sem("up_ready"), sem("down_ready")
        hit_used = sem("hit_used")
        wp_hi_ready, xact_hi_ready, sel_ready = sem("wp_hi_ready"), sem("xact_hi_ready"), sem("sel_ready")
        idx_ready, w_hi_ready, x2T_hi_ready, hf_hi_ready = (sem(n) for n in
            ("idx_ready", "w_hi_ready", "x2T_hi_ready", "hf_hi_ready"))
        a_exp, a_ready = sem("a_exp"), sem("a_ready")
        tap_last, xact_ready, zs_ready = sem("tap_last"), sem("xact_ready"), sem("zs_ready")
        qk_copied, score_copied = sem("qk_copied"), sem("score_copied")
        dtf_copied, dt_biased, sp_abs, sp_exp, sp_ln = (sem(n) for n in
            ("dtf_copied", "dt_biased", "sp_abs", "sp_exp", "sp_ln"))
        abar_ready = sem("abar_ready")
        prob_ready, sg_ready = sem("prob_ready"), sem("sg_ready")
        taps = sem("taps")
        sp_step, step_ready = sem("sp_step"), sem("step_ready")
        du_ready, bu_ready, scanned, ch_ready, yd_ready, y_ready = (sem(n) for n in
            ("du_ready", "bu_ready", "scanned", "ch_ready", "yd_ready", "y_ready"))
        summed, stat_ready, mv_ready, normed = sem("summed"), sem("stat_ready"), sem("mv_ready"), sem("normed")
        weighed, masked, rsum_ready, attended = (sem(n) for n in
            ("weighed", "masked", "rsum_ready", "attended"))
        h_ready, hf_lo_ready, x2T_lo_ready = sem("h_ready"), sem("hf_lo_ready"), sem("x2T_lo_ready")
        hit_ready, w_lo_ready = sem("hit_ready"), sem("w_lo_ready")
        stored = sem("stored")

        block = ctx.enter_context(nc.Block())

        TAPS = K - 1

        def p_used(kind, n):
            return {"x": (taps, TAPS * (n + 1)), "z": (zs_ready, n + 1), "gate": (sg_ready, n + 1)}[kind]

        def q_used(kind, n):
            return {"delta": (du_ready, n + 1), "b": (bu_ready, n + 1), "c": (ch_ready, n + 1),
                    "up": (h_ready, n + 1)}[kind]

        def m_used(kind, n):
            if kind in ("out", "down"):
                return summed, SUMS.index((kind, n)) + 1
            return {"qk": qk_copied, "score": score_copied, "dtf": dtf_copied, "dt": dt_biased,
                    "turn": x2T_lo_ready, "lut": w_lo_ready}[kind], n + 1

        SUMS = [("out", t) for t in range(NT)] + [("down", t) for t in range(NT)]

        def sum_at(kind, t):
            return SUMS.index((kind, t)) + 1

        NORMS = [(k, t) for h in range(NH) for k in (0, 1) for t in range(TH * h, TH * h + TH)] \
            + [(2, t) for t in range(NT)]


        halves = [range(CT * h, CT * (h + 1)) for h in range(NH)]
        P_ORDER = [(kind, u) for u in range(NH * CT) for kind in ("x", "z")] \
            + [("gate", n) for n in range(NH * IT)]
        Q_ORDER = [(kind, u) for u in range(NH * CT)
                   for kind in (("delta", "b", "c") if u else ("b", "c", "delta"))] \
            + [("up", n) for n in range(NH * IT)]
        LUTS = [("lut", c) for c in range(len(CHUNKS))]
        M_ORDER = [("qk", n) for n in range(4)] + [("dtf", 0), ("score", 0), ("dt", 0)] \
            + [("score", b) for b in range(1, NB)] + LUTS[:NCH_IN - 4] + [("dtf", 1), ("dt", 1)] \
            + LUTS[NCH_IN - 4:NCH_IN] + [("out", t) for t in range(TH)] + LUTS[NCH_IN:NCH_IN + 2] \
            + [("out", 4), ("out", 5), ("turn", 0), ("turn", 1), ("out", 6), ("turn", 2), ("out", 7), ("turn", 3)] \
            + LUTS[NCH_IN + 2:] + [("down", 0), ("turn", 4), ("turn", 5), ("down", 1), ("turn", 6), ("turn", 7),
                                   ("down", 2), ("down", 3)] + [("down", t) for t in range(TH, NT)]

        def p_bank(kind, n):
            return pP[P_ORDER.index((kind, n)) % NPB]

        def q_bank(kind, n):
            return pQ[Q_ORDER.index((kind, n)) % NQB]

        def m_bank(kind, n):
            return pM[M_ORDER.index((kind, n)) % NMB]

        @block.sync
        def _(sp_e):
            def load(name, dst, src):
                nc.sync.dma_start(dst, src).then_inc(ld[name], 16)

            by_p = lambda a: a.rearrange("(t p) n -> p t n", p=P)
            load("wx0", wx[:, :, 0:P], by_p(WxT[:, 0:P]))
            load("xt0", xT_sb[:, :, 0:S], by_p(xT[:, 0:S]))
            load("wx1", wx[:, :, P:C], by_p(WxT[:, P:C]))
            load("ch", ch[:, :, :], chan.rearrange("(t p) n -> p t n", p=P))
            load("wz", wz[:, :, :], by_p(WzT))
            load("xt1", xT_sb[:, :, S:T], by_p(xT[:, S:T]))
            for k in range(CT):
                if k >= 2:
                    sp_e.wait_ge(wp_lo_ready, k - 1)
                load(f"wp{k % 2}", wp_in[:, k % 2, :], WpT[k * P:(k + 1) * P, :])
                if k == 1:
                    for q in range(P // G):
                        load("lut", lut_in[q * G:(q + 1) * G, :], lut[J * q:J * q + J].partition_broadcast(G))
                    load("dt", wdt[:, :], WdtT)
                    for q in range(Q):
                        load("dt", bdt[q * H:(q + 1) * H, :], b_dt)
                    load("ctx", ctx_sb[:, :], ctxT)
                    load("ctx", wqk[:, 0, :], WqT)
                    load("ctx", wqk[:, 1, :], WkT)
                    load("ctx", bqk[:, 0:1], bq)
                    load("ctx", bqk[:, 1:2], bk)
                    load("mask", am_u8[:, :, :], by_p(attn_mask))
                    load("mask", km_u8[:, :, :], key_mask.partition_broadcast(P))
            load("wo", wo[:, :, :], by_p(WoT))
            sp_e.wait_ge(z_ready, NH * CT)
            sp_e.wait_ge(wp_lo_ready, CT)
            for c, (w, k, c0, n) in enumerate(CHUNKS):
                if c == 2:
                    sp_e.wait_ge(score_ready, NB)
                    load("x", x_sb[:, :, :], by_p(x))
                if c >= 2:
                    sp_e.wait_ge(idx_ready, c - 1)
                if c == len(CHUNKS) - 1:
                    sp_e.wait_ge(idx_cleared, 1)
                src = (gate_idxT, up_idxT, down_idxT)[w]
                rows = min(P, src.shape[0] - k * P)
                groups = [(0, rows // G, G)] + ([(rows // G, 1, rows % G)] if rows % G else [])
                for g, ng, r in groups:
                    first = k * P + g * G
                    part = src[first:first + ng * r, c0:c0 + n].rearrange("(g r) n -> r g n", r=r)
                    for q in range(P // G):
                        load(f"idx{c % 2}", idx_in[q * G:q * G + r, c % 2, 0:(P // G) * n]
                             .rearrange("p (g n) -> p g n", n=n)[:, g:g + ng, :], part)
            for t in range(NT):
                sp_e.wait_ge(normed, 2 * NT + t + 1)
                nc.sync.dma_start(out[t * P:(t + 1) * P, :], x1[:, t, :]).then_inc(stored, 16)
            sp_e.wait_ge(stored, 16 * NT)

        @block.gpsimd
        def _(pool):
            nc.gpsimd.memset(ident[:, :], 0.0).then_inc(consts_made, 1)
            nc.gpsimd.memset(sel[:, :, :, :], 0.0).then_inc(consts_made, 1)
            nc.gpsimd.memset(qmask[:, :, :], 1.0).then_inc(consts_made, 1)
            nc.gpsimd.memset(mhalf[:, :], -0.5).then_inc(consts_made, 1)
            nc.gpsimd.memset(eye[:, :], 0.0).then_inc(consts_made, 1)
            pool.wait_ge(consts_made, 5)
            nc.gpsimd.affine_select(out=ident[:, :], in_=ident[:, :], compare_op=ALU.not_equal, fill=1.0,
                                    base=0, pattern=[[-1, P]], channel_multiplier=1).then_inc(ident_made, 1)
            for q in range(Q):
                pool.wait_ge(sel_made, q) if q else pool.wait_ge(ident_made, 1)
                rows = sel[q * H:(q + 1) * H, :, :, :].rearrange("p t g n -> p (t g) n")
                nc.gpsimd.affine_select(out=rows, in_=rows, compare_op=ALU.not_equal, fill=1.0, base=0,
                                        pattern=[[-1, H], [0, N]], channel_multiplier=1).then_inc(sel_made, 1)
            pool.wait_ge(sel_made, Q)
            nc.gpsimd.affine_select(out=qmask[:, :, :], in_=qmask[:, :, :], compare_op=ALU.is_ge, fill=0.0,
                                    base=0, pattern=[[-H, Q], [0, P]], channel_multiplier=1).then_inc(qmask_made, 1)
            pool.wait_ge(qmask_made, 1)
            nc.gpsimd.affine_select(out=qmask[:, :, :], in_=qmask[:, :, :], compare_op=ALU.is_ge, fill=0.0,
                                    base=H - 1, pattern=[[H, Q], [0, P]], channel_multiplier=-1)\
                .then_inc(qmask_made, 1)
            pool.wait_ge(qmask_made, 2)
            for q in range(P // G):
                if q:
                    pool.wait_ge(eye_made, q)
                nc.gpsimd.affine_select(out=eye[:, :], in_=eye[:, :], compare_op=ALU.not_equal, fill=1.0,
                                        base=-G * q, pattern=[[-1, G]], channel_multiplier=1).then_inc(eye_made, 1)
            for q in range(P // G):
                pool.wait_ge(eye_made, P // G + q)
                nc.gpsimd.memset(first_entry[q * G:(q + 1) * G, :], float(-J * q)).then_inc(eye_made, 1)
            pool.wait_ge(ld["lut"], 16 * (P // G))
            pool.wait_ge(eye_made, 2 * (P // G))
            rest = lut_in[:, :]
            for k in range(3):
                nc.gpsimd.tensor_copy(lut_part[:, k, :], rest).then_inc(lut_step, 1)
                pool.wait_ge(lut_step, 2 * k + 1)
                if k < 2:
                    nc.gpsimd.tensor_tensor(lut_rest[:, k, :], rest, lut_part[:, k, :], ALU.subtract)\
                        .then_inc(lut_step, 1)
                    pool.wait_ge(lut_step, 2 * k + 2)
                    rest = lut_rest[:, k, :]
            for k in range(3):
                for j in range(J):
                    nc.gpsimd.tensor_scalar(lut_diag[:, k, j, :], eye[:, :], lut_part[:, k, j:j + 1], None,
                                            ALU.mult).then_inc(lut_made, 1)

            def split_xact(u):
                cols = slice((u % CT) * T + (u // CT) * S, (u % CT) * T + (u // CT + 1) * S)
                pool.wait_ge(xact_hi_ready, u + 1)
                nc.gpsimd.tensor_tensor(xact_lo[:, cols], xact[:, u % CT, (u // CT) * S:(u // CT + 1) * S],
                                        value(xact_hi[:, cols]), ALU.subtract).then_inc(xact_lo_ready, 1)

            for u in halves[0]:
                split_xact(u)
            pool.wait_ge(ld["mask"], 32)
            nc.gpsimd.tensor_scalar(am_big[:, :, :], am_u8[:, :, :], MASKED, None, ALU.mult)\
                .then_inc(mask_made, 1)
            nc.gpsimd.tensor_scalar(km_big[:, :, :], km_u8[:, :, :], MASKED, None, ALU.mult)\
                .then_inc(mask_made, 1)
            pool.wait_ge(mask_made, 2)
            for b in range(NB):
                nc.gpsimd.tensor_tensor(mask_big[:, b, :, :], am_big[:, :, :],
                                        km_big[:, b:b + 1, :].to_broadcast([P, LT, L]),
                                        ALU.add).then_inc(mask_made, 1)
            for u in halves[1]:
                split_xact(u)

            def norm_factors(k, t):
                n = NORMS.index((k, t))
                pool.wait_ge(mv_ready, n + 1)
                nc.gpsimd.tensor_scalar(rstd[:, n, 0:1], mv[:, n, 1:2], EPS, None, ALU.add).then_inc(var_eps, 1)
                pool.wait_ge(var_eps, n + 1)
                nc.gpsimd.tensor_tensor(rstd[:, n, 1:2], rstd[:, n, 0:1], mhalf[:, :], ALU.pow)\
                    .then_inc(rstd_made, 1)
                pool.wait_ge(rstd_made, n + 1)
                nc.gpsimd.tensor_scalar(rstd[:, n, 2:3], mv[:, n, 0:1], rstd[:, n, 1:2], -1.0, ALU.mult, ALU.mult)\
                    .then_inc(rstd_ready, 1)

            def gated(u):
                m, cols = u % CT, slice((u // CT) * S, (u // CT + 1) * S)
                pool.wait_ge(yd_ready, u + 1)
                pool.wait_ge(zs_ready, u + 1)
                nc.gpsimd.tensor_tensor(zs[:, m, cols], zs[:, m, cols], hst[:, u % 2, :], ALU.mult)\
                    .then_inc(y_ready, 1)

            def weigh(t):
                pool.wait_ge(normed, NORMS.index((0, t)) + 1)
                nc.gpsimd.tensor_tensor(sc[:, t, :], sc[:, t, :], x1[:, t, :], ALU.mult).then_inc(weighed, 1)

            def no_key(t):
                pool.wait_ge(masked, t + 1)
                nc.gpsimd.tensor_scalar(guard[:, t, 0:1], nmax[:, t:t + 1], MASKED / 2, MASKED, ALU.is_ge, ALU.mult)\
                    .then_inc(guard_step, 1)
                pool.wait_ge(guard_step, 2 * t + 1)
                nc.gpsimd.tensor_tensor(guard[:, t, 1:2], guard[:, t, 0:1], nmax[:, t:t + 1], ALU.mult)\
                    .then_inc(guard_step, 1)
                pool.wait_ge(guard_step, 2 * t + 2)
                nc.gpsimd.tensor_tensor(guard[:, t, 2:3], guard[:, t, 1:2], nmax[:, t:t + 1], ALU.add)\
                    .then_inc(guarded, 1)

            for u in halves[0]:
                gated(u)
            gated(CT)
            for t in (0, 1):
                norm_factors(0, t)
            gated(CT + 1)
            for t in (0, 1):
                weigh(t)
            for t in (2, 3):
                norm_factors(0, t)
            for t in (0, 1):
                no_key(t)
            gated(CT + 2)
            for t in (2, 3):
                weigh(t)
            for t in (0, 1):
                norm_factors(1, t)
            for t in (2, 3):
                no_key(t)
            gated(CT + 3)
            for t in (2, 3):
                norm_factors(1, t)
            for t in range(TH, NT):
                norm_factors(0, t)
            for t in range(TH, NT):
                weigh(t)
            for t in range(TH, NT):
                no_key(t)
            for t in range(TH, NT):
                norm_factors(1, t)
            for t in range(NT):
                norm_factors(2, t)

        @block.tensor
        def _(pe):
            rings = {"P": (pP, P_ORDER, p_used), "Q": (pQ, Q_ORDER, q_used), "M": (pM, M_ORDER, m_used)}

            def bank(r, kind, n):
                banks, order, used = rings[r]
                at, size = order.index((kind, n)), len(banks)
                if at >= size:
                    pe.wait_ge(*used(*order[at - size]))
                return banks[at % size]

            def product(dst, pairs):
                for k, (lhsT, rhs) in enumerate(pairs):
                    last = nc.tensor.matmul(dst, lhsT, rhs, start=(k == 0), stop=(k == len(pairs) - 1))
                return last

            def exact(w, wcols, x, xcols):
                return [(a[:, wcols], b[:, xcols]) for a, b in ((w[0], x[0]), (w[0], x[1]), (w[1], x[0]))]

            wp_k = [[a[:, k, :] for a in (wp_hi, wp_lo)] for k in range(CT)]

            def params(c0, h):
                return [pair for k in range(CT) for pair in exact(
                    wp_k[k], slice(c0, c0 + P), (xact_hi, xact_lo), slice(k * T + h * S, k * T + (h + 1) * S))]

            def project(kind, w, ready, h, m):
                dst = bank("P", kind, CT * h + m)
                product(dst[:, :], [(w[:, k, m * P:(m + 1) * P], xT_sb[:, k, h * S:(h + 1) * S])
                                    for k in range(DT)]).then_inc(ready, 1)

            def step_size(h):
                pe.wait_ge(xact_lo_ready, CT * (h + 1))
                dst = bank("M", "dtf", h)
                product(dst[:, :], params(0, h)).then_inc(dtf_ready, 1)

            def step_heads(h):
                dst = bank("M", "dt", h)
                pe.wait_ge(dtf_copied, h + 1)
                for q in range(Q):
                    last = nc.tensor.matmul(dst[q * H:(q + 1) * H, 0:P], wdt[:, :], dtf[:, q * P:(q + 1) * P],
                                            start=True, stop=True)
                last.then_inc(dt_ready, 1)

            def states(h, m):
                u = CT * h + m

                def delta():
                    dst = bank("Q", "delta", u)
                    pe.wait_ge(step_ready, 2 * (h + 1))
                    product(dst[:, :], [(sel_r[:, m * P:(m + 1) * P], part[:, :]) for part in (step_hi, step_lo)])\
                        .then_inc(delta_ready, 1)

                if u:
                    delta()
                dst = bank("Q", "b", u)
                product(dst[:, :], params(R + m * P, h)).then_inc(b_ready, 1)
                dst = bank("Q", "c", u)
                product(dst[:, :], params(R + C + m * P, h)).then_inc(c_ready, 1)
                if u == 0:
                    decode(0)
                    delta()

            def decode(c):
                w, k, c0, n = CHUNKS[c]
                dst = bank("M", "lut", c)
                for j in range(J):
                    pe.wait_ge(hit_ready, J * c + j + 1)
                    for part in range(3):
                        for g in range(P // G):
                            last = nc.tensor.matmul(dst[g * G:(g + 1) * G, 0:n], lut_diag[:, part, j, :],
                                                    hit[:, j, g * n:(g + 1) * n],
                                                    start=(j == 0 and part == 0),
                                                    stop=(j == J - 1 and part == 2))
                    last.then_inc(hit_used, 1)

            def mix_out(t):
                dst = bank("M", "out", t)
                pe.wait_ge(y_ready, CT * (t // TH + 1))
                product(dst[:, 0:D], [(zs[:, k, t * P:(t + 1) * P], wo[:, k, :]) for k in range(CT)])\
                    .then_inc(out_ready, 1)

            def turn(t):
                dst = bank("M", "turn", t)
                pe.wait_ge(normed, NORMS.index((1, t)) + 1)
                for k in range(DT):
                    last = nc.tensor.transpose(dst[:, k * P:(k + 1) * P], x1[:, t, k * P:(k + 1) * P], ident[:, :])
                last.then_inc(x2T_ready, 1)

            def ffn_in(h, i):
                n = IT * h + i
                if i == 0:
                    pe.wait_ge(x2T_lo_ready, TH * (h + 1))
                    if h == 0:
                        pe.wait_ge(w_lo_ready, NCH_IN)
                        pe.wait_ge(pad_made, 2)
                for r, kind, w, ready in (("P", "gate", 0, gate_ready), ("Q", "up", 1, up_ready)):
                    dst = bank(r, kind, n)
                    product(dst[:, :], [pair for k in range(DT) for pair in exact(
                        [a[:, w, k, :] for a in w_in], slice(i * P, (i + 1) * P),
                        (x2T_hi[:, k, :], x2T_lo[:, k, :]), slice(0, S))]).then_inc(ready, 1)

            def ffn_out(t):
                dst = bank("M", "down", t)
                h, o = t // TH, (t % TH) * P
                for i in range(IT):
                    if t == 0:
                        pe.wait_ge(w_lo_ready, NCH_IN + i + 1)
                    if t % TH == 0:
                        pe.wait_ge(hf_lo_ready, IT * h + i + 1)
                    for n, (lhsT, rhs) in enumerate(exact((hf_hi[:, i, :], hf_lo[:, i, :]), slice(o, o + P),
                                                          [a[:, i, :] for a in w_down], slice(0, D))):
                        last = nc.tensor.matmul(dst[:, 0:D], lhsT, rhs, start=(i + n == 0),
                                                stop=(i == IT - 1 and n == 2))
                last.then_inc(down_ready, 1)

            def query_key(n):
                dst = bank("M", "qk", n)
                product(dst[0:E, :], [(wqk[:, n // 2, :], ctx_sb[:, (n % 2) * S:(n % 2 + 1) * S])])\
                    .then_inc(qk_ready, 1)

            def scores(b):
                dst = bank("M", "score", b)
                for s in range(LT):
                    o = b * L + s * P
                    last = nc.tensor.matmul(dst[:, s * L:(s + 1) * L], qk[:, 0, o:o + P],
                                            qk[:, 1, b * L:(b + 1) * L], start=True, stop=True)
                last.then_inc(score_ready, 1)

            for h in range(NH):
                pe.wait_ge(ld[f"xt{h}"], 16)
                for m in range(CT):
                    if h == 0 and m < 2:
                        pe.wait_ge(ld[f"wx{m}"], 16)
                    project("x", wx, x_ready, h, m)
                    if h == 0 and m == 0:
                        pe.wait_ge(ld["wz"], 16)
                    project("z", wz, z_ready, h, m)
                if h == 0:
                    pe.wait_ge(ld["ctx"], 16 * 5)
                    for n in range(4):
                        query_key(n)
            pe.wait_ge(wp_lo_ready, CT)
            step_size(0)
            pe.wait_ge(qk_copied, 4)
            scores(0)
            pe.wait_ge(ld["dt"], 16 * (1 + Q))
            step_heads(0)
            for b in range(1, NB):
                scores(b)
            pe.wait_ge(sel_ready, 1)
            pe.wait_ge(lut_made, 3 * J)
            for m in range(CT):
                states(0, m)
                if m == CT - 2:
                    step_heads(1)
                if m:
                    decode(2 * m)
                decode(2 * m + 1)
                if m == CT - 3:
                    step_size(1)
            pe.wait_ge(ld["wo"], 16)
            for m in range(CT):
                states(1, m)
                if m < 2:
                    mix_out(2 * m)
                    mix_out(2 * m + 1)
            decode(NCH_IN)
            decode(NCH_IN + 1)
            pe.wait_ge(ident_made, 1)
            mix_out(4)
            mix_out(5)
            turn(0)
            turn(1)
            mix_out(6)
            turn(2)
            mix_out(7)
            turn(3)
            for i in range(IT):
                ffn_in(0, i)
                if i >= 2:
                    decode(NCH_IN + i)
            ffn_out(0)
            turn(4)
            turn(5)
            ffn_out(1)
            turn(6)
            turn(7)
            ffn_out(2)
            ffn_out(3)
            for i in range(IT):
                ffn_in(1, i)
            for t in range(TH, NT):
                ffn_out(t)

        @block.scalar
        def _(act):
            ALOG = K + 2

            def conv_first(u):
                act.wait_ge(x_ready, u + 1)
                if u >= 3:
                    act.wait_ge(xact_ready, u - 2)
                m = u % CT
                nc.scalar.activation(acc[:, u % 3, :], p_bank("x", u)[:, :], ACT.Identity,
                                     bias=ch[:, m, K:K + 1], scale=ch[:, m, K - 1:K]).then_inc(tap_last, 1)

            def conv_silu(u):
                act.wait_ge(taps, TAPS * (u + 1))
                nc.scalar.activation(xact[:, u % CT, (u // CT) * S:(u // CT + 1) * S], acc[:, u % 3, :],
                                     ACT.Silu).then_inc(xact_ready, 1)

            def xact_split(u):
                m, cols = u % CT, slice((u // CT) * S, (u // CT + 1) * S)
                act.wait_ge(xact_ready, u + 1)
                nc.scalar.activation(xact_hi[:, m * T + cols.start:m * T + cols.stop], xact[:, m, cols], ACT.Copy)\
                    .then_inc(xact_hi_ready, 1)

            def wp_split(k):
                act.wait_ge(ld[f"wp{k % 2}"], 16 * (k // 2 + 1))
                nc.scalar.activation(wp_hi[:, k, :], wp_in[:, k % 2, :], ACT.Copy).then_inc(wp_hi_ready, 1)

            def idx_convert(c):
                n = (P // G) * CHUNKS[c][3]
                dmas = [(P // G) * (1 if min(P, (I if CHUNKS[e][0] == 2 else D) - CHUNKS[e][1] * P) % G == 0 else 2)
                        for e in range(c % 2, c + 1, 2)]
                act.wait_ge(ld[f"idx{c % 2}"], 16 * sum(dmas))
                if c >= 2:
                    act.wait_ge(hit_ready, J * (c - 1))
                nc.scalar.activation(idx_rel[:, c % 2, 0:n], idx_in[:, c % 2, 0:n], ACT.Identity,
                                     bias=first_entry[:, 0:1]).then_inc(idx_ready, 1)

            def w_split(c):
                act.wait_ge(hit_used, J * (c + 1))
                nc.scalar.activation(weights(c)[0], m_bank("lut", c)[:, 0:CHUNKS[c][3]], ACT.Copy)\
                    .then_inc(w_hi_ready, 1)

            def z_silu(u):
                act.wait_ge(z_ready, u + 1)
                nc.scalar.activation(zs[:, u % CT, (u // CT) * S:(u // CT + 1) * S], p_bank("z", u)[:, :],
                                     ACT.Silu).then_inc(zs_ready, 1)

            def dtf_copy(h):
                act.wait_ge(dtf_ready, h + 1)
                act.wait_ge(dt_ready, h) if h else act.wait_ge(sel_ready, 1)
                nc.scalar.activation(dtf[:, :], m_bank("dtf", h)[:, :], ACT.Copy).then_inc(dtf_copied, 1)

            def softplus_parts(h):
                act.wait_ge(dt_ready, h + 1)
                if h:
                    act.wait_ge(step_ready, 2 * h)
                nc.scalar.activation(sp[:, 0, :], m_bank("dt", h)[:, 0:P], ACT.Identity, bias=bdt[:, 0:1])\
                    .then_inc(dt_biased, 1)
                act.wait_ge(dt_biased, h + 1)
                nc.scalar.activation(sp[:, 1, :], sp[:, 0, :], ACT.Abs).then_inc(sp_abs, 1)
                act.wait_ge(sp_abs, h + 1)
                nc.scalar.activation(sp[:, 2, :], sp[:, 1, :], ACT.Exp, scale=-1.0).then_inc(sp_exp, 1)
                act.wait_ge(sp_exp, h + 1)
                nc.scalar.activation(sp[:, 3, :], sp[:, 2, :], ACT.Ln, bias=1.0).then_inc(sp_ln, 1)

            def decay(u):
                act.wait_ge(delta_ready, u + 1)
                if u == 0:
                    act.wait_ge(mask_made, 2 + NB)
                if u >= 2:
                    act.wait_ge(scanned, BH * (u - 1))
                nc.scalar.activation(abar[:, u % 2, :], q_bank("delta", u)[:, :], ACT.Exp,
                                     scale=neg_a[:, u % CT:u % CT + 1]).then_inc(abar_ready, 1)

            def prob(t):
                act.wait_ge(guarded, t + 1)
                nc.scalar.activation(sc[:, t, :], sc[:, t, :], ACT.Exp, bias=guard[:, t, 2:3], scale=-1.0,
                                     accum_out=psum_p[:, t:t + 1]).then_inc(prob_ready, 1)

            def turn_split(t):
                act.wait_ge(x2T_ready, t + 1)
                nc.scalar.activation(x2T_hi[:, :, (t % TH) * P:(t % TH + 1) * P],
                                     m_bank("turn", t)[:, 0:DT * P].rearrange("p (k n) -> p k n", k=DT),
                                     ACT.Copy).then_inc(x2T_hi_ready, 1)

            def gate_silu(n):
                act.wait_ge(gate_ready, n + 1)
                if n >= 3:
                    act.wait_ge(hf_lo_ready, n - 2)
                nc.scalar.activation(acc[:, n % 3, :], p_bank("gate", n)[:, :], ACT.Silu).then_inc(sg_ready, 1)

            def hidden_split(n):
                act.wait_ge(h_ready, n + 1)
                if n == IT:
                    act.wait_ge(down_ready, TH)
                nc.scalar.activation(hf_hi[:, n % IT, :], acc[:, n % 3, :], ACT.Copy).then_inc(hf_hi_ready, 1)

            def normalize(k, t):
                n = NORMS.index((k, t))
                act.wait_ge(rstd_ready, n + 1)
                nc.scalar.activation(x1[:, t, :], (sc if k == 1 else x_sb)[:, t, :], ACT.Identity,
                                     bias=rstd[:, n, 2:3], scale=rstd[:, n, 1:2]).then_inc(normed, 1)

            def decoded(c):
                if c + 1 < len(CHUNKS):
                    idx_convert(c + 1)
                w_split(c)

            act.wait_ge(ld["ch"], 16)
            for u in range(NH * CT):
                conv_first(u)
                if u:
                    conv_silu(u - 1)
                    xact_split(u - 1)
                z_silu(u)
                if u in (1, 2):
                    wp_split(u - 1)
                if u in (4, 5):
                    wp_split(u - 2)
                if u == 2:
                    act.wait_ge(sel_made, Q)
                    nc.scalar.activation(sel_r[:, :], sel[:, :, :, :].rearrange("p t g n -> p (t g n)"),
                                         ACT.Copy).then_inc(sel_ready, 1)
                if u == CT - 1:
                    for n in range(4):
                        act.wait_ge(qk_ready, n + 1)
                        nc.scalar.activation(qk[:, n // 2, (n % 2) * S:(n % 2 + 1) * S], m_bank("qk", n)[0:E, :],
                                             ACT.Identity, bias=bqk[:, n // 2:n // 2 + 1]).then_inc(qk_copied, 1)
            conv_silu(NH * CT - 1)
            xact_split(NH * CT - 1)
            dtf_copy(0)

            def score_copy(b):
                act.wait_ge(score_ready, b + 1)
                nc.scalar.activation(sc[:, LT * b:LT * (b + 1), :],
                                     m_bank("score", b)[:, :].rearrange("p (s l) -> p s l", s=LT),
                                     ACT.Copy, scale=-SCALE).then_inc(score_copied, 1)

            score_copy(0)
            nc.scalar.preload_act_table_set("natural_log_exp_and_others")
            act.wait_ge(ld["dt"], 16 * (1 + Q))
            softplus_parts(0)
            score_copy(1)
            act.wait_ge(eye_made, 2 * (P // G))
            idx_convert(0)
            for b in range(2, NB):
                score_copy(b)
            nc.scalar.activation(neg_a[:, :], ch[:, :, ALOG], ACT.Exp).then_inc(a_exp, 1)
            act.wait_ge(a_exp, 1)
            nc.scalar.mul(neg_a[:, :], neg_a[:, :], -1.0).then_inc(a_ready, 1)
            idx_convert(1)
            act.wait_ge(a_ready, 1)
            for m in range(CT):
                decay(m)
                if m:
                    idx_convert(2 * m + 1)
                if m == CT - 2:
                    softplus_parts(1)
                w_split(2 * m)
                decoded(2 * m + 1)
                if m == CT - 3:
                    dtf_copy(1)
            decay(CT)
            decay(CT + 1)
            for t in (0, 1):
                normalize(0, t)
            decay(CT + 2)
            for t in (0, 1):
                prob(t)
            for t in (2, 3):
                normalize(0, t)
            decay(CT + 3)
            for t in (0, 1):
                normalize(1, t)
            decoded(NCH_IN)
            for t in (2, 3):
                prob(t)
            idx_convert(NCH_IN + 2)
            for t in (2, 3):
                normalize(1, t)
            w_split(NCH_IN + 1)
            for pair in ((0, 1), (2, 3)):
                for t in pair:
                    turn_split(t)
                for t in pair:
                    normalize(0, TH + t)
            for t in range(TH, NT):
                prob(t)
            gate_silu(0)
            for n in range(1, IT):
                gate_silu(n)
                hidden_split(n - 1)
                if n <= TH:
                    normalize(1, TH + n - 1)
                if n >= 2:
                    decoded(NCH_IN + n)
            hidden_split(IT - 1)
            for t in range(TH, NT):
                turn_split(t)
            gate_silu(IT)
            for n in range(IT + 1, NH * IT):
                gate_silu(n)
                hidden_split(n - 1)
                if n - IT <= TH:
                    normalize(2, n - IT - 1)
            hidden_split(NH * IT - 1)
            for t in range(TH, NT):
                normalize(2, t)

        @block.vector
        def _(dve):
            def conv_taps(u):
                m = u % CT
                a = acc[:, u % 3, :].rearrange("p (b l) -> p b l", b=BH)
                src = p_bank("x", u)[:, :].rearrange("p (b l) -> p b l", b=BH)
                dve.wait_ge(tap_last, u + 1)
                for k in range(TAPS):
                    back = K - 1 - k
                    if k:
                        dve.wait_ge(taps, TAPS * u + k)
                    nc.vector.scalar_tensor_tensor(out=a[:, :, back:L], in0=src[:, :, 0:L - back],
                                                   scalar=ch[:, m, k:k + 1], in1=a[:, :, back:L],
                                                   op0=ALU.mult, op1=ALU.add).then_inc(taps, 1)

            def softplus(h):
                base = 6 * h
                dve.wait_ge(sp_exp, h + 1)
                nc.vector.tensor_scalar(sp[:, 4, :], sp[:, 2, :], 1.0, -1.0, ALU.add, ALU.add).then_inc(sp_step, 1)
                dve.wait_ge(sp_step, base + 1)
                nc.vector.tensor_tensor(sp[:, 4, :], sp[:, 2, :], sp[:, 4, :], ALU.subtract).then_inc(sp_step, 1)
                dve.wait_ge(sp_step, base + 2)
                dve.wait_ge(sp_ln, h + 1)
                nc.vector.tensor_tensor(sp[:, 4, :], sp[:, 4, :], sp[:, 3, :], ALU.add).then_inc(sp_step, 1)
                dve.wait_ge(sp_step, base + 3)
                nc.vector.scalar_tensor_tensor(out=sp[:, 1, :], in0=sp[:, 0, :], scalar=0.0, in1=sp[:, 4, :],
                                               op0=ALU.max, op1=ALU.add).then_inc(sp_step, 1)
                dve.wait_ge(sp_step, base + 4)
                nc.vector.tensor_copy(sp_hi[:, :], sp[:, 1, :]).then_inc(sp_step, 1)
                dve.wait_ge(sp_step, base + 5)
                nc.vector.tensor_tensor(sp[:, 2, :], sp[:, 1, :], value(sp_hi[:, :]), ALU.subtract)\
                    .then_inc(sp_step, 1)

            def spread(h):
                dve.wait_ge(sp_step, 6 * (h + 1))
                dve.wait_ge(qmask_made, 2)
                if h:
                    dve.wait_ge(delta_ready, CT * h)
                for dst, src in ((step_hi, value(sp_hi[:, :]).unsqueeze(1)), (step_lo, sp[:, 2:3, :])):
                    nc.vector.tensor_tensor(dst[:, :].rearrange("p (q n) -> p q n", q=Q), qmask[:, :, :],
                                            src.to_broadcast([P, Q, P]), ALU.mult).then_inc(step_ready, 1)

            def state_space(u):
                m, h, s = u % CT, u // CT, u % 2
                cols = slice(h * S, (h + 1) * S)
                dve.wait_ge(delta_ready, u + 1)
                dve.wait_ge(abar_ready, u + 1)
                if u >= 2:
                    dve.wait_ge(y_ready, u - 1)
                nc.vector.tensor_tensor(du[:, s, :], q_bank("delta", u)[:, :], xact[:, m, cols], ALU.mult)\
                    .then_inc(du_ready, 1)
                dve.wait_ge(du_ready, u + 1)
                dve.wait_ge(b_ready, u + 1)
                nc.vector.tensor_tensor(du[:, s, :], q_bank("b", u)[:, :], du[:, s, :], ALU.mult)\
                    .then_inc(bu_ready, 1)
                dve.wait_ge(bu_ready, u + 1)
                for b in range(BH):
                    c = slice(b * L, (b + 1) * L)
                    nc.vector.tensor_tensor_scan(hst[:, s, c], abar[:, s, c], du[:, s, c], 0.0,
                                                 ALU.mult, ALU.add).then_inc(scanned, 1)
                dve.wait_ge(scanned, BH * (u + 1))
                dve.wait_ge(c_ready, u + 1)
                nc.vector.tensor_tensor(hst[:, s, :], q_bank("c", u)[:, :], hst[:, s, :], ALU.mult)\
                    .then_inc(ch_ready, 1)
                dve.wait_ge(ch_ready, u + 1)
                nc.vector.scalar_tensor_tensor(out=hst[:, s, :], in0=xact[:, m, cols], scalar=ch[:, m, K + 1:K + 2],
                                               in1=hst[:, s, :], op0=ALU.mult, op1=ALU.add).then_inc(yd_ready, 1)

            def norm_stats(k, tiles, src):
                for t in tiles:
                    dve.wait_ge(attended, t + 1) if k == 1 else dve.wait_ge(summed, sum_at(("out", 0, "down")[k], t))
                    nc.vector.bn_stats(stats[:, NORMS.index((k, t)), :], src[:, t, :]).then_inc(stat_ready, 1)
                for t in tiles:
                    n = NORMS.index((k, t))
                    dve.wait_ge(stat_ready, n + 1)
                    nc.vector.bn_aggr(mv[:, n, :], stats[:, n, :]).then_inc(mv_ready, 1)

            def mixed(tiles):
                for t in tiles:
                    dve.wait_ge(out_ready, t + 1)
                    nc.vector.tensor_tensor(x_sb[:, t, :], m_bank("out", t)[:, 0:D], x_sb[:, t, :], ALU.add)\
                        .then_inc(summed, 1)
                norm_stats(0, tiles, x_sb)

            def mask(tiles):
                for t in tiles:
                    dve.wait_ge(weighed, t + 1)
                    nc.vector.tensor_tensor_reduce(out=sc[:, t, :], in0=sc[:, t, :],
                                                   in1=mask_big[:, t // LT, t % LT, :],
                                                   scale=1.0, scalar=3e38, op0=ALU.add, op1=ALU.min,
                                                   accum_out=nmax[:, t:t + 1]).then_inc(masked, 1)

            def attend(tiles):
                for t in tiles:
                    dve.wait_ge(prob_ready, t + 1)
                    nc.vector.reciprocal(rsum[:, t:t + 1], psum_p[:, t:t + 1]).then_inc(rsum_ready, 1)
                for t in tiles:
                    dve.wait_ge(rsum_ready, t + 1)
                    nc.vector.scalar_tensor_tensor(out=sc[:, t, :], in0=sc[:, t, :], scalar=rsum[:, t:t + 1],
                                                   in1=x1[:, t, :], op0=ALU.mult, op1=ALU.add).then_inc(attended, 1)
                norm_stats(1, tiles, sc)

            def hidden(n):
                dve.wait_ge(sg_ready, n + 1)
                dve.wait_ge(up_ready, n + 1)
                nc.vector.tensor_tensor(acc[:, n % 3, :], q_bank("up", n)[:, :], acc[:, n % 3, :], ALU.mult)\
                    .then_inc(h_ready, 1)

            def hidden_rest(n):
                dve.wait_ge(hf_hi_ready, n + 1)
                nc.vector.tensor_tensor(hf_lo[:, n % IT, :], acc[:, n % 3, :], value(hf_hi[:, n % IT, :]),
                                        ALU.subtract).then_inc(hf_lo_ready, 1)

            def turn_rest(t):
                cols = slice((t % TH) * P, (t % TH + 1) * P)
                dve.wait_ge(x2T_hi_ready, t + 1)
                nc.vector.tensor_tensor(x2T_lo[:, :, cols],
                                        m_bank("turn", t)[:, 0:DT * P].rearrange("p (k n) -> p k n", k=DT),
                                        value(x2T_hi[:, :, cols]), ALU.subtract).then_inc(x2T_lo_ready, 1)

            def ffn_sum(t):
                dve.wait_ge(down_ready, t + 1)
                nc.vector.tensor_tensor(x1[:, t, :], m_bank("down", t)[:, 0:D], x1[:, t, :], ALU.add)\
                    .then_inc(summed, 1)
                norm_stats(2, (t,), x1)

            def hits(c):
                n = (P // G) * CHUNKS[c][3]
                dve.wait_ge(idx_ready, c + 1)
                for j in range(J):
                    if c:
                        dve.wait_ge(hit_used, J * (c - 1) + j + 1)
                    nc.vector.tensor_scalar(hit[:, j, 0:n], idx_rel[:, c % 2, 0:n], float(j), None,
                                            ALU.is_equal).then_inc(hit_ready, 1)
                if c == len(CHUNKS) - 3:
                    nc.vector.memset(idx_in[:, c % 2, D:(P // G) * D], 2 * V).then_inc(idx_cleared, 1)

            def w_rest(c):
                hi, lo = weights(c)
                dve.wait_ge(w_hi_ready, c + 1)
                nc.vector.tensor_tensor(lo, m_bank("lut", c)[:, 0:CHUNKS[c][3]], value(hi), ALU.subtract)\
                    .then_inc(w_lo_ready, 1)

            for a in w_in:
                nc.vector.memset(value(a[:, :, :, I:IP]), 0.0).then_inc(pad_made, 1)
            def wp_rest(k):
                dve.wait_ge(wp_hi_ready, k + 1)
                nc.vector.tensor_tensor(wp_lo[:, k, :], wp_in[:, k % 2, :], value(wp_hi[:, k, :]), ALU.subtract)\
                    .then_inc(wp_lo_ready, 1)

            def decoding(c):
                if c + 1 < len(CHUNKS):
                    hits(c + 1)
                w_rest(c)

            dve.wait_ge(ld["ch"], 16)
            for u in range(NH * CT):
                conv_taps(u)
                if u in (1, 2):
                    wp_rest(u - 1)
                if u in (4, 5):
                    wp_rest(u - 2)
            hits(0)
            softplus(0)
            spread(0)
            decoding(0)
            for m in range(CT):
                state_space(m)
                if m == CT - 1:
                    spread(1)
                if m:
                    decoding(2 * m)
                if m == CT - 2:
                    softplus(1)
                decoding(2 * m + 1)
            dve.wait_ge(ld["x"], 16)
            dve.wait_ge(mask_made, 2 + NB)
            state_space(CT)
            mixed((0, 1))
            state_space(CT + 1)
            mask((0, 1))
            mixed((2, 3))
            state_space(CT + 2)
            attend((0, 1))
            mask((2, 3))
            state_space(CT + 3)
            decoding(NCH_IN)
            attend((2, 3))
            decoding(NCH_IN + 1)
            mixed((4, 5))
            turn_rest(0)
            turn_rest(1)
            mixed((6,))
            turn_rest(2)
            mixed((7,))
            turn_rest(3)
            mask(range(TH, NT))
            hidden(0)
            for n in range(1, IT):
                if n <= TH:
                    attend((TH + n - 1,))
                hidden(n)
                hidden_rest(n - 1)
                if n >= 2:
                    decoding(NCH_IN + n)
            hidden_rest(IT - 1)
            ffn_sum(0)
            turn_rest(4)
            turn_rest(5)
            ffn_sum(1)
            turn_rest(6)
            turn_rest(7)
            ffn_sum(2)
            ffn_sum(3)
            hidden(IT)
            for n in range(IT + 1, NH * IT):
                hidden(n)
                hidden_rest(n - 1)
            hidden_rest(NH * IT - 1)
            for t in range(TH, NT):
                ffn_sum(t)


def kernel(**inputs):
    import numpy as np
    import concourse.bacc as bacc
    from concourse import mybir as mb
    from concourse.bass_utils import run_bass_kernel_spmd

    a = {n: np.asarray(v) for n, v in inputs.items()}
    B, L, D = a["x"].shape
    flat = a["x"].reshape(B * L, D)
    pre = "L0_attn_"
    C = a[pre + "W_in_x"].shape[0]
    col = lambda n: a[n].reshape(-1, 1)
    device = {
        "x": flat, "xT": flat.T,
        "WxT": a[pre + "W_in_x"].T, "WzT": a[pre + "W_in_z"].T,
        "chan": np.concatenate([a[pre + "conv_w"].reshape(C, -1), col(pre + "conv_b"), col(pre + "D"),
                                col(pre + "A_log")], axis=1),
        "WpT": a[pre + "W_param"].T, "WdtT": a[pre + "W_dt"].T, "b_dt": col(pre + "b_dt"),
        "WoT": a[pre + "W_out"].T,
        "ctxT": a["ctx_512"].reshape(B * L, -1).T,
        "WqT": a["L0_xattn_Wq"].T, "WkT": a["L0_xattn_Wk"].T,
        "bq": col("L0_xattn_bq"), "bk": col("L0_xattn_bk"),
        "attn_mask": a["mask_SxS2_bk1"], "key_mask": a["mask_BxS2_bf0"],
        "lut": a["L0_ffn_lut"], "gate_idxT": a["L0_ffn_gate_idx"].T, "up_idxT": a["L0_ffn_up_idx"].T,
        "down_idxT": a["L0_ffn_down_idx"].T,
    }
    nc = bacc.Bacc("TRN2", target_bir_lowering=False, num_devices=1)
    arrays, args = {}, []
    for name, v in device.items():
        v = np.ascontiguousarray(v)
        arrays[f"in_{name}"] = v
        args.append(nc.dram_tensor(f"in_{name}", v.shape, mb.dt.from_np(v.dtype), kind="ExternalInput").ap())
    args.append(nc.dram_tensor("out_y", (B * L, D), mb.dt.float32, kind="ExternalOutput").ap())
    post_norm_decoder_layer(nc, *args)
    r = run_bass_kernel_spmd(nc, [arrays], core_ids=[0])
    return r.results[0]["out_y"].reshape(B, L, D)
```

```python
import concourse.bass as bass
from concourse import mybir
from contextlib import ExitStack


def post_norm_decoder_layer(nc: bass.Bass, x, xT, WxT, WzT, chan, WpT, WdtT, b_dt, WoT,
                            ctxT, WqT, WkT, bq, bk, attn_mask, key_mask,
                            lut, gate_idxT, up_idxT, down_idxT, out):
    f32, bf16, f32r = mybir.dt.float32, mybir.dt.bfloat16, mybir.dt.float32r
    i32, u8 = mybir.dt.int32, mybir.dt.uint8
    ALU, ACT = mybir.AluOpType, mybir.ActivationFunctionType

    P = 128
    T, D = x.shape
    C = WxT.shape[1]
    R, H = WdtT.shape
    N = C // H
    NB = key_mask.shape[0]
    L = T // NB
    E = ctxT.shape[0]
    I = gate_idxT.shape[1]
    V = lut.shape[0]
    K = 4
    CT, DT, IT = C // P, D // P, -(-I // P)
    IP = IT * P
    NH = 2
    S = T // NH
    BH = NB // NH
    NT, TH = T // P, S // P
    LT = L // P
    Q = P // H
    SCALE = float(E) ** -0.5
    EPS = 1e-5
    MASKED = 1e38
    NPB, NQB, NMB = 3, 3, 2

    ctx = ExitStack()
    with ctx:
        G = 32
        J = V // (P // G)
        IC = I // 2
        CHUNKS = [(w, k, c, IC) for w in (0, 1) for k in range(DT) for c in (0, IC)] \
            + [(2, i, 0, D) for i in range(IT)]
        CH = (P // G) * IC
        NCH_IN = 2 * DT * 2

        def sb(name, shape, dt=f32):
            return ctx.enter_context(nc.sbuf_tensor(name, shape, dt))

        def sem(name):
            return ctx.enter_context(nc.semaphore(name))

        WPC = R + 2 * C
        early = sb("early", [P, max(DT * T + 2 * DT * C + 2 * WPC, (J + 2) * CH // 2 + 2 * CH)])
        xT_sb = early[:, 0:DT * T].rearrange("p (k t) -> p k t", k=DT)
        wx, wz = (early[:, at:at + DT * C].rearrange("p (k c) -> p k c", k=DT)
                  for at in (DT * T, DT * T + DT * C))
        wp_in = early[:, DT * T + 2 * DT * C:DT * T + 2 * DT * C + 2 * WPC].rearrange("p (s c) -> p s c", s=2)
        hit = early[:, 0:J * CH // 2].bitcast(bf16).rearrange("p (j n) -> p j n", j=J)
        idx_rel = early[:, J * CH // 2:(J + 2) * CH // 2].bitcast(bf16).rearrange("p (s n) -> p s n", s=2)
        idx_in = early[:, (J + 2) * CH // 2:(J + 2) * CH // 2 + 2 * CH].bitcast(i32)\
            .rearrange("p (s n) -> p s n", s=2)
        x_sb = sb("x_sb", [P, NT, D])
        wdt = sb("wdt", [R, H])
        ch = sb("ch", [P, CT, K + 3])
        bdt = sb("bdt", [P, 1])
        du = sb("du", [P, 2, S])
        ctx_sb = du[0:E, :, :].rearrange("p s n -> p (s n)")
        bqk = sb("bqk", [E, 2])
        am_u8 = sb("am_u8", [P, LT, L], u8)
        km_u8 = sb("km_u8", [P, NB, L], u8)
        lut_in = sb("lut_in", [P, J])
        wp_hi, wp_lo = (sb(n, [P, CT, R + 2 * C], f32r) for n in ("wp_hi", "wp_lo"))
        wo_hi, wo_lo = (sb(n, [P, CT, D], f32r) for n in ("wo_hi", "wo_lo"))
        w_in = [sb(n, [P, 2, DT, IP], f32r) for n in ("w_in_hi", "w_in_lo")]
        w_down = [a[:, :, :].rearrange("p k n -> p (k n)")[:, 0:IT * D].rearrange("p (i n) -> p i n", i=IT)
                  for a in (wp_hi, wp_lo)]

        def weights(c):
            w, k, c0, n = CHUNKS[c]
            return [a[:, k, :] for a in w_down] if w == 2 else [a[:, w, k, c0:c0 + n] for a in w_in]

        first_entry = sb("first_entry", [P, 1])
        eye = sb("eye", [P, G], bf16)
        lut_rest = sb("lut_rest", [P, 2, J])
        lut_part = sb("lut_part", [P, 3, J], bf16)
        lut_diag = sb("lut_diag", [P, 3, J, G], bf16)
        ident = sb("ident", [P, P])
        dtf = sb("dtf", [R, S])
        sel = dtf[:, :].rearrange("p (t g n) -> p t g n", t=CT, n=N)
        sel_r = sb("sel_r", [P, C], f32r)
        qmask = sb("qmask", [P, Q, P], bf16)
        neg_a = sb("neg_a", [P, CT])
        qk = x_sb[0:E, :, :].rearrange("p (a t) d -> p a (t d)", a=2)
        sc = sb("sc", [P, NT, L])
        sc_flat = sc[:, :, :].rearrange("p t l -> p (t l)")
        wqk = sc_flat[0:E, 0:2 * E].rearrange("p (w e) -> p w e", w=2)
        wo_at = NT * L - CT * D
        wo_in = sc_flat[:, wo_at:].rearrange("p (k d) -> p k d", k=CT)
        abar = sb("abar", [P, 2, S])
        big = abar[:, :, :].rearrange("p s n -> p (s n)").bitcast(bf16)
        am_big = big[:, 0:LT * L].rearrange("p (s l) -> p s l", s=LT)
        km_big = big[:, LT * L:(LT + NB) * L].rearrange("p (b l) -> p b l", b=NB)
        mask_big = sb("mask_big", [P, NB, LT, L], bf16)
        acc = sb("acc", [P, 3, S])
        xact = sb("xact", [P, CT, T])
        xact_hi, xact_lo = (sb(n, [P, CT * T], f32r) for n in ("xact_hi", "xact_lo"))
        zs = sb("zs", [P, CT, T])
        sp = acc[:, :, :].rearrange("p a s -> p (a s)")[:, 0:5 * P].rearrange("p (a n) -> p a n", a=5)
        sp_hi = sb("sp_hi", [P, P], f32r)
        step_hi, step_lo = (sb(n, [P, S], f32r) for n in ("step_hi", "step_lo"))
        hst = du
        x1 = x_sb
        stats = sb("stats", [P, 3 * NT, 6])
        mv = sb("mv", [P, 3 * NT, 2])
        rstd = sb("rstd", [P, 3 * NT, 3])
        mhalf = sb("mhalf", [P, 1])
        nmax = sb("nmax", [P, NT])
        psum_p = sb("psum_p", [P, NT])
        rsum = sb("rsum", [P, NT])
        guard = sb("guard", [P, NT, 3])
        y_hi, y_lo = (a[:, :].rearrange("p (m t) -> p m t", m=CT)[:, :, 0:S] for a in (xact_hi, xact_lo))
        hf_hi, hf_lo = (a[:, 0:IT * S].rearrange("p (i t) -> p i t", i=IT) for a in (xact_hi, xact_lo))
        x2T_hi, x2T_lo = (a[:, :, :].rearrange("p k n -> p (k n)")[:, IT * D:IT * D + DT * S]
                          .rearrange("p (k t) -> p k t", k=DT) for a in (wp_hi, wp_lo))
        flat_in = [a[:, :, :, :].rearrange("p w k n -> p (w k n)") for a in w_in]
        xT_hi, xT_lo = (a[:, 0:DT * T].rearrange("p (k t) -> p k t", k=DT) for a in flat_in)
        wx_hi, wz_hi = (a[:, DT * T:DT * (T + C)].rearrange("p (k c) -> p k c", k=DT) for a in flat_in)
        wx_lo, wz_lo = (xact_lo[:, :].rearrange("p (m t) -> p m t", m=CT)[:, at:at + DT, S:S + C]
                        for at in (0, DT))

        def value(a):
            return a.bitcast(f32)

        pP = [ctx.enter_context(nc.psum_tensor(f"pP{i}", [P, S], f32)) for i in range(NPB)]
        pQ = [ctx.enter_context(nc.psum_tensor(f"pQ{i}", [P, S], f32)) for i in range(NQB)]
        pM = [ctx.enter_context(nc.psum_tensor(f"pM{i}", [P, S], f32)) for i in range(NMB)]

        ld = {n: sem("ld_" + n) for n in
              ("wx0", "wx1", "xt0_0", "xt0_1", "xt1", "ch", "wz", "dt", "wp0", "wp1", "ctx", "mask", "lut",
               "idx0", "idx1", "wo", "x")}
        consts_made = sem("consts_made")
        ident_made = sem("ident_made")
        sel_made = sem("sel_made")
        qmask_made, pad_made = sem("qmask_made"), sem("pad_made")
        mask_made = sem("mask_made")
        eye_made, lut_step, lut_made = sem("eye_made"), sem("lut_step"), sem("lut_made")
        wp_lo_ready, xact_lo_ready = sem("wp_lo_ready"), sem("xact_lo_ready")
        xt0_hi_ready, wx_hi_ready, wz_hi_ready, xt1_hi_ready, in_lo_ready, xt1_lo_ready = (sem(n) for n in
            ("xt0_hi_ready", "wx_hi_ready", "wz_hi_ready", "xt1_hi_ready", "in_lo_ready", "xt1_lo_ready"))
        idx_cleared, y_lo_ready, y_last_lo_ready = sem("idx_cleared"), sem("y_lo_ready"), sem("y_last_lo_ready")
        wo_hi_ready, wo_lo_ready = sem("wo_hi_ready"), sem("wo_lo_ready")
        var_eps = sem("var_eps")
        rstd_made, rstd_ready = sem("rstd_made"), sem("rstd_ready")
        guard_step, guarded = sem("guard_step"), sem("guarded")
        x_ready, z_ready = sem("x_ready"), sem("z_ready")
        qk_ready, score_ready = sem("qk_ready"), sem("score_ready")
        dtf_ready, dt_ready = sem("dtf_ready"), sem("dt_ready")
        delta_ready, b_ready, c_ready = sem("delta_ready"), sem("b_ready"), sem("c_ready")
        out_ready, x2T_ready = sem("out_ready"), sem("x2T_ready")
        gate_ready, up_ready, down_ready = sem("gate_ready"), sem("up_ready"), sem("down_ready")
        hit_used = sem("hit_used")
        wp_hi_ready, xact_hi_ready, sel_ready = sem("wp_hi_ready"), sem("xact_hi_ready"), sem("sel_ready")
        idx_ready, w_hi_ready, x2T_hi_ready, hf_hi_ready = (sem(n) for n in
            ("idx_ready", "w_hi_ready", "x2T_hi_ready", "hf_hi_ready"))
        a_exp, a_ready = sem("a_exp"), sem("a_ready")
        tap_last, xact_ready, zs_ready = sem("tap_last"), sem("xact_ready"), sem("zs_ready")
        qk_copied, score_copied = sem("qk_copied"), sem("score_copied")
        dtf_copied, dt_biased, sp_abs, sp_exp, sp_ln = (sem(n) for n in
            ("dtf_copied", "dt_biased", "sp_abs", "sp_exp", "sp_ln"))
        abar_ready, y_hi_ready = sem("abar_ready"), sem("y_hi_ready")
        prob_ready, sg_ready = sem("prob_ready"), sem("sg_ready")
        taps = sem("taps")
        sp_step, step_ready = sem("sp_step"), sem("step_ready")
        du_ready, bu_ready, scanned, ch_ready, yd_ready, y_ready = (sem(n) for n in
            ("du_ready", "bu_ready", "scanned", "ch_ready", "yd_ready", "y_ready"))
        summed, stat_ready, mv_ready, normed = sem("summed"), sem("stat_ready"), sem("mv_ready"), sem("normed")
        finished = sem("finished")
        weighed, masked, rsum_ready, attended = (sem(n) for n in
            ("weighed", "masked", "rsum_ready", "attended"))
        h_ready, hf_lo_ready, x2T_lo_ready = sem("h_ready"), sem("hf_lo_ready"), sem("x2T_lo_ready")
        hit_ready, w_lo_ready = sem("hit_ready"), sem("w_lo_ready")
        stored = sem("stored")

        block = ctx.enter_context(nc.Block())

        TAPS = K - 1

        def bank_used(kind, n):
            if kind in ("out", "down"):
                return summed, SUMS.index((kind, n)) + 1
            if kind == "x":
                return taps, TAPS * (n + 1)
            return {"z": zs_ready, "gate": sg_ready, "delta": du_ready, "b": bu_ready, "c": ch_ready,
                    "up": h_ready, "qk": qk_copied, "score": score_copied, "dtf": dtf_copied,
                    "dt": dt_biased, "turn": x2T_lo_ready, "lut": w_lo_ready}[kind], n + 1

        SUMS = [("out", t) for t in range(NT)] + [("down", t) for t in range(NT)]

        def sum_at(kind, t):
            return SUMS.index((kind, t)) + 1

        NORMS = [(k, t) for h in range(NH) for k in (0, 1) for t in range(TH * h, TH * h + TH)] \
            + [(2, t) for t in range(NT)]

        halves = [range(CT * h, CT * (h + 1)) for h in range(NH)]
        some = lambda kind, first, end: [(kind, n) for n in range(first, end)]
        CH_ALL = len(CHUNKS)
        RINGS = {
            "P": (pP, some("x", 0, NH * CT) + some("c", 0, NH * CT) + some("out", TH, NT - 1)
                  + some("gate", 0, IT) + [("down", 1), ("turn", 4), ("turn", 5), ("turn", 6)]
                  + some("gate", IT, NH * IT) + [("down", 5), ("down", 7)]),
            "Q": (pQ, some("z", 0, NH * CT) + some("score", 0, NB)
                  + [(kind, u) for u in range(NH * CT)
                       for kind in (("delta", "b") if u else ("b", "delta"))]
                  + some("turn", 0, TH) + some("up", 0, IT) + [("down", 3)] + some("up", IT, NH * IT)),
            "M": (pM, some("qk", 0, 4) + [("dtf", 0), ("dt", 0)] + some("lut", 0, NCH_IN - 4)
                  + [("dtf", 1), ("dt", 1)] + some("lut", NCH_IN - 4, NCH_IN)
                  + some("out", 0, TH) + some("lut", NCH_IN, NCH_IN + 2) + some("out", NT - 1, NT)
                  + some("lut", NCH_IN + 2, CH_ALL)
                  + [("down", 0), ("down", 2), ("turn", 7), ("down", 4), ("down", 6)]),
        }

        def filled(kind, n):
            for banks, order in RINGS.values():
                if (kind, n) in order:
                    return banks, order, order.index((kind, n))

        def bank_of(kind, n):
            banks, _, at = filled(kind, n)
            return banks[at % len(banks)]

        @block.sync
        def _(sp_e):
            def load(name, dst, src):
                nc.sync.dma_start(dst, src).then_inc(ld[name], 16)

            by_p = lambda a: a.rearrange("(t p) n -> p t n", p=P)
            load("wx0", wx[:, :, 0:P], by_p(WxT[:, 0:P]))
            for k in range(DT):
                load(f"xt0_{k}", xT_sb[:, k, 0:S], xT[k * P:(k + 1) * P, 0:S])
            load("wx1", wx[:, :, P:C], by_p(WxT[:, P:C]))
            load("ch", ch[:, :, :], chan.rearrange("(t p) n -> p t n", p=P))
            load("wz", wz[:, :, :], by_p(WzT))
            load("xt1", xT_sb[:, :, S:T], by_p(xT[:, S:T]))
            for k in range(CT):
                if k >= 2:
                    sp_e.wait_ge(wp_lo_ready, k - 1)
                load(f"wp{k % 2}", wp_in[:, k % 2, :], WpT[k * P:(k + 1) * P, :])
                if k == 1:
                    for q in range(P // G):
                        load("lut", lut_in[q * G:(q + 1) * G, :], lut[J * q:J * q + J].partition_broadcast(G))
                    load("dt", wdt[:, :], WdtT)
                    for q in range(Q):
                        load("dt", bdt[q * H:(q + 1) * H, :], b_dt)
                    load("ctx", ctx_sb[:, :], ctxT)
                    load("ctx", wqk[:, 0, :], WqT)
                    load("ctx", wqk[:, 1, :], WkT)
                    load("ctx", bqk[:, 0:1], bq)
                    load("ctx", bqk[:, 1:2], bk)
                    load("mask", am_u8[:, :, :], by_p(attn_mask))
                    load("mask", km_u8[:, :, :], key_mask.partition_broadcast(P))
            load("wo", wo_in, by_p(WoT))
            sp_e.wait_ge(z_ready, NH * CT)
            sp_e.wait_ge(wp_lo_ready, CT)
            for c, (w, k, c0, n) in enumerate(CHUNKS):
                if c == 2:
                    sp_e.wait_ge(score_ready, NB)
                    load("x", x_sb[:, :, :], by_p(x))
                if c >= 2:
                    sp_e.wait_ge(idx_ready, c - 1)
                if c == len(CHUNKS) - 1:
                    sp_e.wait_ge(idx_cleared, 1)
                src = (gate_idxT, up_idxT, down_idxT)[w]
                rows = min(P, src.shape[0] - k * P)
                groups = [(0, rows // G, G)] + ([(rows // G, 1, rows % G)] if rows % G else [])
                for g, ng, r in groups:
                    first = k * P + g * G
                    part = src[first:first + ng * r, c0:c0 + n].rearrange("(g r) n -> r g n", r=r)
                    for q in range(P // G):
                        load(f"idx{c % 2}", idx_in[q * G:q * G + r, c % 2, 0:(P // G) * n]
                             .rearrange("p (g n) -> p g n", n=n)[:, g:g + ng, :], part)
            for t in range(NT):
                sp_e.wait_ge(finished, t + 1)
                nc.sync.dma_start(out[t * P:(t + 1) * P, :], x1[:, t, :]).then_inc(stored, 16)
            sp_e.wait_ge(stored, 16 * NT)

        @block.gpsimd
        def _(pool):
            nc.gpsimd.memset(ident[:, :], 0.0).then_inc(consts_made, 1)
            nc.gpsimd.memset(sel[:, :, :, :], 0.0).then_inc(consts_made, 1)
            nc.gpsimd.memset(qmask[:, :, :], 1.0).then_inc(consts_made, 1)
            nc.gpsimd.memset(mhalf[:, :], -0.5).then_inc(consts_made, 1)
            nc.gpsimd.memset(eye[:, :], 0.0).then_inc(consts_made, 1)
            pool.wait_ge(consts_made, 5)
            nc.gpsimd.affine_select(out=ident[:, :], in_=ident[:, :], compare_op=ALU.not_equal, fill=1.0,
                                    base=0, pattern=[[-1, P]], channel_multiplier=1).then_inc(ident_made, 1)
            for q in range(Q):
                pool.wait_ge(sel_made, q) if q else pool.wait_ge(ident_made, 1)
                rows = sel[q * H:(q + 1) * H, :, :, :].rearrange("p t g n -> p (t g) n")
                nc.gpsimd.affine_select(out=rows, in_=rows, compare_op=ALU.not_equal, fill=1.0, base=0,
                                        pattern=[[-1, H], [0, N]], channel_multiplier=1).then_inc(sel_made, 1)
            pool.wait_ge(sel_made, Q)
            nc.gpsimd.affine_select(out=qmask[:, :, :], in_=qmask[:, :, :], compare_op=ALU.is_ge, fill=0.0,
                                    base=0, pattern=[[-H, Q], [0, P]], channel_multiplier=1).then_inc(qmask_made, 1)
            pool.wait_ge(qmask_made, 1)
            nc.gpsimd.affine_select(out=qmask[:, :, :], in_=qmask[:, :, :], compare_op=ALU.is_ge, fill=0.0,
                                    base=H - 1, pattern=[[H, Q], [0, P]], channel_multiplier=-1)\
                .then_inc(qmask_made, 1)
            pool.wait_ge(qmask_made, 2)
            for q in range(P // G):
                if q:
                    pool.wait_ge(eye_made, q)
                nc.gpsimd.affine_select(out=eye[:, :], in_=eye[:, :], compare_op=ALU.not_equal, fill=1.0,
                                        base=-G * q, pattern=[[-1, G]], channel_multiplier=1).then_inc(eye_made, 1)
            for q in range(P // G):
                pool.wait_ge(eye_made, P // G + q)
                nc.gpsimd.memset(first_entry[q * G:(q + 1) * G, :], float(-J * q)).then_inc(eye_made, 1)
            pool.wait_ge(eye_made, 2 * (P // G))
            pool.wait_ge(ld["xt1"], 16)
            nc.gpsimd.tensor_copy(xT_hi[:, :, S:T], xT_sb[:, :, S:T]).then_inc(xt1_hi_ready, 1)
            pool.wait_ge(xt1_hi_ready, 1)
            nc.gpsimd.tensor_tensor(xT_lo[:, :, S:T], xT_sb[:, :, S:T], value(xT_hi[:, :, S:T]),
                                    ALU.subtract).then_inc(xt1_lo_ready, 1)
            pool.wait_ge(ld["lut"], 16 * (P // G))
            pool.wait_ge(eye_made, 2 * (P // G))
            rest = lut_in[:, :]
            for k in range(3):
                nc.gpsimd.tensor_copy(lut_part[:, k, :], rest).then_inc(lut_step, 1)
                pool.wait_ge(lut_step, 2 * k + 1)
                if k < 2:
                    nc.gpsimd.tensor_tensor(lut_rest[:, k, :], rest, lut_part[:, k, :], ALU.subtract)\
                        .then_inc(lut_step, 1)
                    pool.wait_ge(lut_step, 2 * k + 2)
                    rest = lut_rest[:, k, :]
            for k in range(3):
                for j in range(J):
                    nc.gpsimd.tensor_scalar(lut_diag[:, k, j, :], eye[:, :], lut_part[:, k, j:j + 1], None,
                                            ALU.mult).then_inc(lut_made, 1)

            def split_xact(u):
                cols = slice((u % CT) * T + (u // CT) * S, (u % CT) * T + (u // CT + 1) * S)
                pool.wait_ge(xact_hi_ready, u + 1)
                if u == CT:
                    pool.wait_ge(z_ready, NH * CT)
                nc.gpsimd.tensor_tensor(xact_lo[:, cols], xact[:, u % CT, (u // CT) * S:(u // CT + 1) * S],
                                        value(xact_hi[:, cols]), ALU.subtract).then_inc(xact_lo_ready, 1)

            for u in halves[0]:
                split_xact(u)
            pool.wait_ge(ld["mask"], 32)
            nc.gpsimd.tensor_scalar(am_big[:, :, :], am_u8[:, :, :], MASKED, None, ALU.mult)\
                .then_inc(mask_made, 1)
            nc.gpsimd.tensor_scalar(km_big[:, :, :], km_u8[:, :, :], MASKED, None, ALU.mult)\
                .then_inc(mask_made, 1)
            pool.wait_ge(mask_made, 2)
            for b in range(NB):
                nc.gpsimd.tensor_tensor(mask_big[:, b, :, :], am_big[:, :, :],
                                        km_big[:, b:b + 1, :].to_broadcast([P, LT, L]),
                                        ALU.add).then_inc(mask_made, 1)
            for u in halves[1]:
                split_xact(u)

            def norm_factors(k, t):
                n = NORMS.index((k, t))
                pool.wait_ge(mv_ready, n + 1)
                nc.gpsimd.tensor_scalar(rstd[:, n, 0:1], mv[:, n, 1:2], EPS, None, ALU.add).then_inc(var_eps, 1)
                pool.wait_ge(var_eps, n + 1)
                nc.gpsimd.tensor_tensor(rstd[:, n, 1:2], rstd[:, n, 0:1], mhalf[:, :], ALU.pow)\
                    .then_inc(rstd_made, 1)
                if k == 2:
                    return
                pool.wait_ge(rstd_made, n + 1)
                nc.gpsimd.tensor_scalar(rstd[:, n, 2:3], mv[:, n, 0:1], rstd[:, n, 1:2], -1.0, ALU.mult, ALU.mult)\
                    .then_inc(rstd_ready, 1)

            def gated(u):
                m, cols = u % CT, slice((u // CT) * S, (u // CT + 1) * S)
                pool.wait_ge(yd_ready, u + 1)
                pool.wait_ge(zs_ready, u + 1)
                nc.gpsimd.tensor_tensor(zs[:, m, cols], zs[:, m, cols], hst[:, u % 2, :], ALU.mult)\
                    .then_inc(y_ready, 1)

            def y_rest(u):
                pool.wait_ge(y_hi_ready, u + 1)
                nc.gpsimd.tensor_tensor(y_lo[:, u % CT, :], zs[:, u % CT, (u // CT) * S:(u // CT + 1) * S],
                                        value(y_hi[:, u % CT, :]), ALU.subtract).then_inc(y_lo_ready, 1)

            def weigh(t):
                pool.wait_ge(normed, NORMS.index((0, t)) + 1)
                nc.gpsimd.tensor_tensor(sc[:, t, :], sc[:, t, :], x1[:, t, :], ALU.mult).then_inc(weighed, 1)

            def no_key(t):
                pool.wait_ge(masked, t + 1)
                nc.gpsimd.tensor_scalar(guard[:, t, 0:1], nmax[:, t:t + 1], MASKED / 2, MASKED, ALU.is_ge, ALU.mult)\
                    .then_inc(guard_step, 1)
                pool.wait_ge(guard_step, 2 * t + 1)
                nc.gpsimd.tensor_tensor(guard[:, t, 1:2], guard[:, t, 0:1], nmax[:, t:t + 1], ALU.mult)\
                    .then_inc(guard_step, 1)
                pool.wait_ge(guard_step, 2 * t + 2)
                nc.gpsimd.tensor_tensor(guard[:, t, 2:3], guard[:, t, 1:2], nmax[:, t:t + 1], ALU.add)\
                    .then_inc(guarded, 1)

            for u in halves[0]:
                gated(u)
            for u in halves[0]:
                y_rest(u)
            gated(CT)
            for t in (0, 1):
                norm_factors(0, t)
            gated(CT + 1)
            for t in (0, 1):
                weigh(t)
            y_rest(CT)
            y_rest(CT + 1)
            for t in (2, 3):
                norm_factors(0, t)
            for t in (0, 1):
                no_key(t)
            gated(CT + 2)
            for t in (2, 3):
                weigh(t)
            y_rest(CT + 2)
            for t in (0, 1):
                norm_factors(1, t)
            for t in (2, 3):
                no_key(t)
            gated(CT + 3)
            for t in (2, 3):
                norm_factors(1, t)
            c = len(CHUNKS) - 1
            pool.wait_ge(idx_ready, c - 1)
            nc.gpsimd.memset(idx_in[:, c % 2, D:(P // G) * D], 2 * V).then_inc(idx_cleared, 1)
            for t in range(TH, NT):
                norm_factors(0, t)
            for t in range(TH, NT):
                weigh(t)
            for t in range(TH, NT):
                no_key(t)
            for t in range(TH, NT):
                norm_factors(1, t)
            for t in range(NT):
                norm_factors(2, t)

        @block.tensor
        def _(pe):
            def bank(kind, n):
                banks, order, at = filled(kind, n)
                if at >= len(banks):
                    pe.wait_ge(*bank_used(*order[at - len(banks)]))
                return banks[at % len(banks)]

            def product(dst, pairs):
                for k, (lhsT, rhs) in enumerate(pairs):
                    last = nc.tensor.matmul(dst, lhsT, rhs, start=(k == 0), stop=(k == len(pairs) - 1))
                return last

            def exact(w, wcols, x, xcols):
                return [(a[:, wcols], b[:, xcols]) for a, b in ((w[0], x[0]), (w[0], x[1]), (w[1], x[0]))]

            wp_k = [[a[:, k, :] for a in (wp_hi, wp_lo)] for k in range(CT)]

            def params(c0, h):
                return [pair for k in range(CT) for pair in exact(
                    wp_k[k], slice(c0, c0 + P), (xact_hi, xact_lo), slice(k * T + h * S, k * T + (h + 1) * S))]

            def project(kind, w, ready, h, m):
                dst = bank(kind, CT * h + m)
                wc, xc = slice(m * P, (m + 1) * P), slice(h * S, (h + 1) * S)
                if h == 0 and m == 0:
                    for k in range(DT):
                        if kind == "x":
                            pe.wait_ge(ld[f"xt0_{k}"], 16)
                            if k == 0:
                                pe.wait_ge(ld["wx0"], 16)
                        last = nc.tensor.matmul(dst[:, :], w[0][:, k, wc], xT_sb[:, k, xc],
                                                start=(k == 0), stop=(k == DT - 1))
                    last.then_inc(ready, 1)
                    return
                pairs = [pair for k in range(DT) for pair in exact(
                    [a[:, k, :] for a in w[1:]], wc, (xT_hi[:, k, :], xT_lo[:, k, :]), xc)]
                product(dst[:, :], pairs).then_inc(ready, 1)

            def step_size(h):
                pe.wait_ge(xact_lo_ready, CT * (h + 1))
                dst = bank("dtf", h)
                product(dst[:, :], params(0, h)).then_inc(dtf_ready, 1)

            def step_heads(h):
                dst = bank("dt", h)
                pe.wait_ge(dtf_copied, h + 1)
                for q in range(Q):
                    last = nc.tensor.matmul(dst[q * H:(q + 1) * H, 0:P], wdt[:, :], dtf[:, q * P:(q + 1) * P],
                                            start=True, stop=True)
                last.then_inc(dt_ready, 1)

            def states(h, m):
                u = CT * h + m

                def delta():
                    dst = bank("delta", u)
                    pe.wait_ge(step_ready, 2 * (h + 1))
                    product(dst[:, :], [(sel_r[:, m * P:(m + 1) * P], part[:, :]) for part in (step_hi, step_lo)])\
                        .then_inc(delta_ready, 1)

                if u:
                    delta()
                dst = bank("b", u)
                product(dst[:, :], params(R + m * P, h)).then_inc(b_ready, 1)
                dst = bank("c", u)
                product(dst[:, :], params(R + C + m * P, h)).then_inc(c_ready, 1)
                if u == 0:
                    decode(0)
                    delta()

            def decode(c):
                w, k, c0, n = CHUNKS[c]
                dst = bank("lut", c)
                for j in range(J):
                    pe.wait_ge(hit_ready, J * c + j + 1)
                    for part in range(3):
                        for g in range(P // G):
                            last = nc.tensor.matmul(dst[g * G:(g + 1) * G, 0:n], lut_diag[:, part, j, :],
                                                    hit[:, j, g * n:(g + 1) * n],
                                                    start=(j == 0 and part == 0),
                                                    stop=(j == J - 1 and part == 2))
                    last.then_inc(hit_used, 1)

            def mix_out(t, tiles=range(CT)):
                dst = bank("out", t) if tiles[0] == 0 else bank_of("out", t)
                h, tokens = t // TH, slice((t % TH) * P, (t % TH + 1) * P)
                if h and tiles[-1] == CT - 1:
                    pe.wait_ge(y_last_lo_ready, 1)
                else:
                    pe.wait_ge(y_lo_ready, CT * h + tiles[-1] + 1)
                for k in tiles:
                    for n, (lhsT, rhs) in enumerate(exact((y_hi[:, k, :], y_lo[:, k, :]), tokens,
                                                          (wo_hi[:, k, :], wo_lo[:, k, :]), slice(0, D))):
                        last = nc.tensor.matmul(dst[:, 0:D], lhsT, rhs, start=(k + n == 0),
                                                stop=(k == CT - 1 and n == 2))
                if tiles[-1] == CT - 1:
                    last.then_inc(out_ready, 1)

            def turn(t):
                dst = bank("turn", t)
                pe.wait_ge(normed, NORMS.index((1, t)) + 1)
                for k in range(DT):
                    last = nc.tensor.transpose(dst[:, k * P:(k + 1) * P], x1[:, t, k * P:(k + 1) * P], ident[:, :])
                last.then_inc(x2T_ready, 1)

            def ffn_in(h, i):
                n = IT * h + i
                if i == 0:
                    pe.wait_ge(x2T_lo_ready, TH * (h + 1))
                    if h == 0:
                        pe.wait_ge(w_lo_ready, NCH_IN)
                        pe.wait_ge(pad_made, 2)
                for kind, w, ready in (("gate", 0, gate_ready), ("up", 1, up_ready)):
                    dst = bank(kind, n)
                    product(dst[:, :], [pair for k in range(DT) for pair in exact(
                        [a[:, w, k, :] for a in w_in], slice(i * P, (i + 1) * P),
                        (x2T_hi[:, k, :], x2T_lo[:, k, :]), slice(0, S))]).then_inc(ready, 1)

            def ffn_out(t, tiles=range(IT)):
                dst = bank("down", t) if tiles[0] == 0 else bank_of("down", t)
                h, o = t // TH, (t % TH) * P
                for i in tiles:
                    if t == 0:
                        pe.wait_ge(w_lo_ready, NCH_IN + i + 1)
                    if t % TH == 0:
                        pe.wait_ge(hf_lo_ready, IT * h + i + 1)
                    for n, (lhsT, rhs) in enumerate(exact((hf_hi[:, i, :], hf_lo[:, i, :]), slice(o, o + P),
                                                          [a[:, i, :] for a in w_down], slice(0, D))):
                        last = nc.tensor.matmul(dst[:, 0:D], lhsT, rhs, start=(i + n == 0),
                                                stop=(i == IT - 1 and n == 2))
                if tiles[-1] == IT - 1:
                    last.then_inc(down_ready, 1)

            def ffn_out_two(t):
                for tiles in (range(IT - 2), range(IT - 2, IT)):
                    for s in (t, t + 1):
                        ffn_out(s, tiles)

            def query_key(n):
                dst = bank("qk", n)
                product(dst[0:E, :], [(wqk[:, n // 2, :], ctx_sb[:, (n % 2) * S:(n % 2 + 1) * S])])\
                    .then_inc(qk_ready, 1)

            def scores(b):
                dst = bank("score", b)
                for s in range(LT):
                    o = b * L + s * P
                    last = nc.tensor.matmul(dst[:, s * L:(s + 1) * L], qk[:, 0, o:o + P],
                                            qk[:, 1, b * L:(b + 1) * L], start=True, stop=True)
                last.then_inc(score_ready, 1)

            for h in range(NH):
                if h == 1:
                    pe.wait_ge(xt1_lo_ready, 1)
                for m in range(CT):
                    if h == 0 and m == 1:
                        pe.wait_ge(in_lo_ready, 2)
                    project("x", (wx, wx_hi, wx_lo), x_ready, h, m)
                    if h == 0 and m == 0:
                        pe.wait_ge(ld["wz"], 16)
                    if h == 0 and m == 1:
                        pe.wait_ge(in_lo_ready, 3)
                    project("z", (wz, wz_hi, wz_lo), z_ready, h, m)
                    n = CT * h + m - (CT - 1)
                    if n == 0:
                        pe.wait_ge(ld["ctx"], 16 * 5)
                    if 0 <= n < 4:
                        query_key(n)
            pe.wait_ge(wp_lo_ready, CT)
            step_size(0)
            pe.wait_ge(qk_copied, 4)
            scores(0)
            scores(1)
            pe.wait_ge(ld["dt"], 16 * (1 + Q))
            step_heads(0)
            scores(2)
            scores(3)
            pe.wait_ge(sel_ready, 1)
            pe.wait_ge(lut_made, 3 * J)
            for m in range(CT):
                states(0, m)
                if m == CT - 2:
                    step_heads(1)
                if m:
                    decode(2 * m)
                decode(2 * m + 1)
                if m == CT - 3:
                    step_size(1)
            pe.wait_ge(wo_lo_ready, 1)
            early_k, last_k = range(CT - 1), range(CT - 1, CT)
            for m in range(CT):
                states(1, m)
                if m == 0:
                    for tiles in (early_k, last_k):
                        mix_out(0, tiles)
                        mix_out(1, tiles)
                if m == 1:
                    mix_out(2)
                    mix_out(3)
                if m == 2:
                    decode(NCH_IN)
            decode(NCH_IN + 1)
            mix_out(4, early_k)
            mix_out(5, early_k)
            pe.wait_ge(ident_made, 1)
            turn(0)
            turn(1)
            mix_out(6, early_k)
            for t in (4, 5, 6):
                mix_out(t, last_k)
            mix_out(7)
            turn(2)
            turn(3)
            decode(NCH_IN + 2)
            for i in range(IT):
                ffn_in(0, i)
                if i >= 3:
                    decode(NCH_IN + i)
            ffn_out_two(0)
            turn(4)
            turn(5)
            ffn_out(2)
            turn(6)
            turn(7)
            ffn_out(3)
            for i in range(IT):
                ffn_in(1, i)
            ffn_out_two(TH)
            for t in range(TH + 2, NT):
                ffn_out(t)

        @block.scalar
        def _(act):
            ALOG = K + 2

            def conv_first(u):
                act.wait_ge(x_ready, u + 1)
                if u >= 3:
                    act.wait_ge(xact_ready, u - 2)
                m = u % CT
                nc.scalar.activation(acc[:, u % 3, :], bank_of("x", u)[:, :], ACT.Identity,
                                     bias=ch[:, m, K:K + 1], scale=ch[:, m, K - 1:K]).then_inc(tap_last, 1)

            def conv_silu(u):
                act.wait_ge(taps, TAPS * (u + 1))
                nc.scalar.activation(xact[:, u % CT, (u // CT) * S:(u // CT + 1) * S], acc[:, u % 3, :],
                                     ACT.Silu).then_inc(xact_ready, 1)

            def xact_split(u):
                m, cols = u % CT, slice((u // CT) * S, (u // CT + 1) * S)
                act.wait_ge(xact_ready, u + 1)
                nc.scalar.activation(xact_hi[:, m * T + cols.start:m * T + cols.stop], xact[:, m, cols], ACT.Copy)\
                    .then_inc(xact_hi_ready, 1)

            def wp_split(k):
                act.wait_ge(ld[f"wp{k % 2}"], 16 * (k // 2 + 1))
                nc.scalar.activation(wp_hi[:, k, :], wp_in[:, k % 2, :], ACT.Copy).then_inc(wp_hi_ready, 1)

            def idx_convert(c):
                n = (P // G) * CHUNKS[c][3]
                dmas = [(P // G) * (1 if min(P, (I if CHUNKS[e][0] == 2 else D) - CHUNKS[e][1] * P) % G == 0 else 2)
                        for e in range(c % 2, c + 1, 2)]
                act.wait_ge(ld[f"idx{c % 2}"], 16 * sum(dmas))
                if c >= 2:
                    act.wait_ge(hit_ready, J * (c - 1))
                nc.scalar.activation(idx_rel[:, c % 2, 0:n], idx_in[:, c % 2, 0:n], ACT.Identity,
                                     bias=first_entry[:, 0:1]).then_inc(idx_ready, 1)

            def w_split(c):
                act.wait_ge(hit_used, J * (c + 1))
                nc.scalar.activation(weights(c)[0], bank_of("lut", c)[:, 0:CHUNKS[c][3]], ACT.Copy)\
                    .then_inc(w_hi_ready, 1)

            def z_silu(u):
                act.wait_ge(z_ready, u + 1)
                nc.scalar.activation(zs[:, u % CT, (u // CT) * S:(u // CT + 1) * S], bank_of("z", u)[:, :],
                                     ACT.Silu).then_inc(zs_ready, 1)

            def dtf_copy(h):
                act.wait_ge(dtf_ready, h + 1)
                act.wait_ge(dt_ready, h) if h else act.wait_ge(sel_ready, 1)
                nc.scalar.activation(dtf[:, :], bank_of("dtf", h)[:, :], ACT.Copy).then_inc(dtf_copied, 1)

            def softplus_parts(h):
                act.wait_ge(dt_ready, h + 1)
                act.wait_ge(step_ready, 2 * h) if h else act.wait_ge(xact_ready, NH * CT)
                nc.scalar.activation(sp[:, 0, :], bank_of("dt", h)[:, 0:P], ACT.Identity, bias=bdt[:, 0:1])\
                    .then_inc(dt_biased, 1)
                act.wait_ge(dt_biased, h + 1)
                nc.scalar.activation(sp[:, 1, :], sp[:, 0, :], ACT.Abs).then_inc(sp_abs, 1)
                act.wait_ge(sp_abs, h + 1)
                nc.scalar.activation(sp[:, 2, :], sp[:, 1, :], ACT.Exp, scale=-1.0).then_inc(sp_exp, 1)
                act.wait_ge(sp_exp, h + 1)
                nc.scalar.activation(sp[:, 3, :], sp[:, 2, :], ACT.Ln, bias=1.0).then_inc(sp_ln, 1)

            def decay(u):
                act.wait_ge(delta_ready, u + 1)
                if u == 0:
                    act.wait_ge(mask_made, 2 + NB)
                if u >= 2:
                    act.wait_ge(scanned, BH * (u - 1))
                nc.scalar.activation(abar[:, u % 2, :], bank_of("delta", u)[:, :], ACT.Exp,
                                     scale=neg_a[:, u % CT:u % CT + 1]).then_inc(abar_ready, 1)

            def y_split(u):
                act.wait_ge(y_ready, u + 1)
                if u == 0:
                    act.wait_ge(c_ready, CT)
                if u == CT:
                    act.wait_ge(out_ready, TH)
                nc.scalar.activation(y_hi[:, u % CT, :], zs[:, u % CT, (u // CT) * S:(u // CT + 1) * S],
                                     ACT.Copy).then_inc(y_hi_ready, 1)

            def prob(t):
                act.wait_ge(guarded, t + 1)
                nc.scalar.activation(sc[:, t, :], sc[:, t, :], ACT.Exp, bias=guard[:, t, 2:3], scale=-1.0,
                                     accum_out=psum_p[:, t:t + 1]).then_inc(prob_ready, 1)

            def turn_split(t):
                act.wait_ge(x2T_ready, t + 1)
                nc.scalar.activation(x2T_hi[:, :, (t % TH) * P:(t % TH + 1) * P],
                                     bank_of("turn", t)[:, 0:DT * P].rearrange("p (k n) -> p k n", k=DT),
                                     ACT.Copy).then_inc(x2T_hi_ready, 1)

            def gate_silu(n):
                act.wait_ge(gate_ready, n + 1)
                if n == 0:
                    act.wait_ge(step_ready, 2 * NH)
                if n >= 3:
                    act.wait_ge(hf_lo_ready, n - 2)
                nc.scalar.activation(acc[:, n % 3, :], bank_of("gate", n)[:, :], ACT.Silu).then_inc(sg_ready, 1)

            def hidden_split(n):
                act.wait_ge(h_ready, n + 1)
                if n == IT:
                    act.wait_ge(down_ready, TH)
                nc.scalar.activation(hf_hi[:, n % IT, :], acc[:, n % 3, :], ACT.Copy).then_inc(hf_hi_ready, 1)

            def normalize(k, t):
                n = NORMS.index((k, t))
                act.wait_ge(rstd_ready, n + 1)
                nc.scalar.activation(x1[:, t, :], (sc if k == 1 else x_sb)[:, t, :], ACT.Identity,
                                     bias=rstd[:, n, 2:3], scale=rstd[:, n, 1:2]).then_inc(normed, 1)

            def decoded(c):
                w_split(c)
                if c + 2 < len(CHUNKS):
                    idx_convert(c + 2)

            nc.scalar.preload_act_table_set("silu_and_others")
            act.wait_ge(ld["wx0"], 16)
            act.wait_ge(ld["wx1"], 16)
            nc.scalar.activation(wx_hi, wx[:, :, :], ACT.Copy).then_inc(wx_hi_ready, 1)
            act.wait_ge(ld["ch"], 16)
            for u in range(NH * CT):
                conv_first(u)
                if u:
                    conv_silu(u - 1)
                    xact_split(u - 1)
                z_silu(u)
                if u in (1, 2):
                    wp_split(u - 1)
                if u in (4, 5):
                    wp_split(u - 2)
                n = u - (CT - 1)
                if 0 <= n < 4:
                    act.wait_ge(qk_ready, n + 1)
                    nc.scalar.activation(qk[:, n // 2, (n % 2) * S:(n % 2 + 1) * S], bank_of("qk", n)[0:E, :],
                                         ACT.Identity, bias=bqk[:, n // 2:n // 2 + 1]).then_inc(qk_copied, 1)
            dtf_copy(0)
            conv_silu(NH * CT - 1)
            xact_split(NH * CT - 1)

            nc.scalar.preload_act_table_set("natural_log_exp_and_others")
            act.wait_ge(ld["dt"], 16 * (1 + Q))
            softplus_parts(0)
            act.wait_ge(eye_made, 2 * (P // G))
            idx_convert(0)
            nc.scalar.activation(neg_a[:, :], ch[:, :, ALOG], ACT.Exp).then_inc(a_exp, 1)
            act.wait_ge(a_exp, 1)
            nc.scalar.mul(neg_a[:, :], neg_a[:, :], -1.0).then_inc(a_ready, 1)
            idx_convert(1)
            act.wait_ge(a_ready, 1)
            for m in range(CT):
                decay(m)
                if m == CT - 2:
                    softplus_parts(1)
                if m == CT - 1:
                    for u in (0, 1, 2):
                        y_split(u)
                decoded(2 * m)
                if m < CT - 1:
                    decoded(2 * m + 1)
                if m == CT - 3:
                    dtf_copy(1)
            w_split(NCH_IN - 1)
            y_split(3)
            decay(CT)
            idx_convert(NCH_IN + 1)
            decay(CT + 1)
            for t in (0, 1):
                normalize(0, t)
            decay(CT + 2)
            y_split(4)
            y_split(5)
            for t in (2, 3):
                normalize(0, t)
            for t in (0, 1):
                prob(t)
            decay(CT + 3)
            y_split(6)
            w_split(NCH_IN)
            for t in (0, 1):
                normalize(1, t)
            for t in (2, 3):
                prob(t)
            w_split(NCH_IN + 1)
            y_split(7)
            idx_convert(NCH_IN + 2)
            for t in (0, 1):
                turn_split(t)
            for t in (2, 3):
                normalize(1, t)
            for t in (2, 3):
                turn_split(t)
            idx_convert(NCH_IN + 3)
            nc.scalar.preload_act_table_set("silu_and_others")
            for t in (4, 5):
                normalize(0, t)
            decoded(NCH_IN + 2)
            gate_silu(0)
            for t in (6, 7):
                normalize(0, t)
            gate_silu(1)
            hidden_split(0)
            nc.scalar.preload_act_table_set("natural_log_exp_and_others")
            for t in range(TH, NT):
                prob(t)
            nc.scalar.preload_act_table_set("silu_and_others")
            for n in range(2, IT):
                gate_silu(n)
                hidden_split(n - 1)
                if n == IT - 1:
                    hidden_split(n)
                if n >= 3:
                    decoded(NCH_IN + n)
                if n >= 4:
                    normalize(1, n)
            normalize(1, 6)
            turn_split(4)
            turn_split(5)
            normalize(1, 7)
            turn_split(6)
            turn_split(7)
            gate_silu(IT)
            for n in range(IT + 1, NH * IT):
                gate_silu(n)
                hidden_split(n - 1)
            hidden_split(NH * IT - 1)

        @block.vector
        def _(dve):
            def conv_taps(u):
                m = u % CT
                a = acc[:, u % 3, :].rearrange("p (b l) -> p b l", b=BH)
                src = bank_of("x", u)[:, :].rearrange("p (b l) -> p b l", b=BH)
                dve.wait_ge(tap_last, u + 1)
                for k in range(TAPS):
                    back = K - 1 - k
                    if k:
                        dve.wait_ge(taps, TAPS * u + k)
                    nc.vector.scalar_tensor_tensor(out=a[:, :, back:L], in0=src[:, :, 0:L - back],
                                                   scalar=ch[:, m, k:k + 1], in1=a[:, :, back:L],
                                                   op0=ALU.mult, op1=ALU.add).then_inc(taps, 1)

            def softplus(h):
                base = 6 * h
                dve.wait_ge(sp_exp, h + 1)
                nc.vector.tensor_scalar(sp[:, 4, :], sp[:, 2, :], 1.0, -1.0, ALU.add, ALU.add).then_inc(sp_step, 1)
                dve.wait_ge(sp_step, base + 1)
                nc.vector.tensor_tensor(sp[:, 4, :], sp[:, 2, :], sp[:, 4, :], ALU.subtract).then_inc(sp_step, 1)
                dve.wait_ge(sp_step, base + 2)
                dve.wait_ge(sp_ln, h + 1)
                nc.vector.tensor_tensor(sp[:, 4, :], sp[:, 4, :], sp[:, 3, :], ALU.add).then_inc(sp_step, 1)
                dve.wait_ge(sp_step, base + 3)
                nc.vector.scalar_tensor_tensor(out=sp[:, 1, :], in0=sp[:, 0, :], scalar=0.0, in1=sp[:, 4, :],
                                               op0=ALU.max, op1=ALU.add).then_inc(sp_step, 1)
                dve.wait_ge(sp_step, base + 4)
                nc.vector.tensor_copy(sp_hi[:, :], sp[:, 1, :]).then_inc(sp_step, 1)
                dve.wait_ge(sp_step, base + 5)
                nc.vector.tensor_tensor(sp[:, 2, :], sp[:, 1, :], value(sp_hi[:, :]), ALU.subtract)\
                    .then_inc(sp_step, 1)

            def spread(h):
                dve.wait_ge(sp_step, 6 * (h + 1))
                dve.wait_ge(qmask_made, 2)
                if h:
                    dve.wait_ge(delta_ready, CT * h)
                for dst, src in ((step_hi, value(sp_hi[:, :]).unsqueeze(1)), (step_lo, sp[:, 2:3, :])):
                    nc.vector.tensor_tensor(dst[:, :].rearrange("p (q n) -> p q n", q=Q), qmask[:, :, :],
                                            src.to_broadcast([P, Q, P]), ALU.mult).then_inc(step_ready, 1)

            def state_in(u):
                m, h, s = u % CT, u // CT, u % 2
                cols = slice(h * S, (h + 1) * S)
                dve.wait_ge(delta_ready, u + 1)
                dve.wait_ge(abar_ready, u + 1)
                if u >= 2:
                    dve.wait_ge(y_ready, u - 1)
                nc.vector.tensor_tensor(du[:, s, :], bank_of("delta", u)[:, :], xact[:, m, cols], ALU.mult)\
                    .then_inc(du_ready, 1)
                dve.wait_ge(du_ready, u + 1)
                dve.wait_ge(b_ready, u + 1)
                nc.vector.tensor_tensor(du[:, s, :], bank_of("b", u)[:, :], du[:, s, :], ALU.mult)\
                    .then_inc(bu_ready, 1)
                dve.wait_ge(bu_ready, u + 1)
                for b in range(BH):
                    c = slice(b * L, (b + 1) * L)
                    nc.vector.tensor_tensor_scan(hst[:, s, c], abar[:, s, c], du[:, s, c], 0.0,
                                                 ALU.mult, ALU.add).then_inc(scanned, 1)

            def state_out(u):
                m, h, s = u % CT, u // CT, u % 2
                cols = slice(h * S, (h + 1) * S)
                dve.wait_ge(scanned, BH * (u + 1))
                dve.wait_ge(c_ready, u + 1)
                nc.vector.tensor_tensor(hst[:, s, :], bank_of("c", u)[:, :], hst[:, s, :], ALU.mult)\
                    .then_inc(ch_ready, 1)
                dve.wait_ge(ch_ready, u + 1)
                nc.vector.scalar_tensor_tensor(out=hst[:, s, :], in0=xact[:, m, cols], scalar=ch[:, m, K + 1:K + 2],
                                               in1=hst[:, s, :], op0=ALU.mult, op1=ALU.add).then_inc(yd_ready, 1)

            def state_space(u):
                state_in(u)
                state_out(u)

            def norm_stats(k, tiles, src):
                for t in tiles:
                    dve.wait_ge(attended, t + 1) if k == 1 else dve.wait_ge(summed, sum_at(("out", 0, "down")[k], t))
                    nc.vector.bn_stats(stats[:, NORMS.index((k, t)), :], src[:, t, :]).then_inc(stat_ready, 1)
                for t in tiles:
                    n = NORMS.index((k, t))
                    dve.wait_ge(stat_ready, n + 1)
                    nc.vector.bn_aggr(mv[:, n, :], stats[:, n, :]).then_inc(mv_ready, 1)

            def mixed(tiles):
                for t in tiles:
                    dve.wait_ge(out_ready, t + 1)
                    nc.vector.tensor_tensor(x_sb[:, t, :], bank_of("out", t)[:, 0:D], x_sb[:, t, :], ALU.add)\
                        .then_inc(summed, 1)
                norm_stats(0, tiles, x_sb)

            def mask(tiles):
                for t in tiles:
                    dve.wait_ge(weighed, t + 1)
                    nc.vector.tensor_tensor_reduce(out=sc[:, t, :], in0=sc[:, t, :],
                                                   in1=mask_big[:, t // LT, t % LT, :],
                                                   scale=1.0, scalar=3e38, op0=ALU.add, op1=ALU.min,
                                                   accum_out=nmax[:, t:t + 1]).then_inc(masked, 1)

            def attend(tiles):
                for t in tiles:
                    dve.wait_ge(prob_ready, t + 1)
                    nc.vector.reciprocal(rsum[:, t:t + 1], psum_p[:, t:t + 1]).then_inc(rsum_ready, 1)
                for t in tiles:
                    dve.wait_ge(rsum_ready, t + 1)
                    nc.vector.scalar_tensor_tensor(out=sc[:, t, :], in0=sc[:, t, :], scalar=rsum[:, t:t + 1],
                                                   in1=x1[:, t, :], op0=ALU.mult, op1=ALU.add).then_inc(attended, 1)
                norm_stats(1, tiles, sc)

            def hidden(n):
                dve.wait_ge(sg_ready, n + 1)
                dve.wait_ge(up_ready, n + 1)
                nc.vector.tensor_tensor(acc[:, n % 3, :], bank_of("up", n)[:, :], acc[:, n % 3, :], ALU.mult)\
                    .then_inc(h_ready, 1)

            def hidden_rest(n):
                dve.wait_ge(hf_hi_ready, n + 1)
                nc.vector.tensor_tensor(hf_lo[:, n % IT, :], acc[:, n % 3, :], value(hf_hi[:, n % IT, :]),
                                        ALU.subtract).then_inc(hf_lo_ready, 1)

            def turn_rest(t):
                cols = slice((t % TH) * P, (t % TH + 1) * P)
                dve.wait_ge(x2T_hi_ready, t + 1)
                nc.vector.tensor_tensor(x2T_lo[:, :, cols],
                                        bank_of("turn", t)[:, 0:DT * P].rearrange("p (k n) -> p k n", k=DT),
                                        value(x2T_hi[:, :, cols]), ALU.subtract).then_inc(x2T_lo_ready, 1)

            def ffn_sum(t):
                dve.wait_ge(down_ready, t + 1)
                nc.vector.tensor_tensor(x1[:, t, :], bank_of("down", t)[:, 0:D], x1[:, t, :], ALU.add)\
                    .then_inc(summed, 1)
                norm_stats(2, (t,), x1)

            def finish(t):
                n = NORMS.index((2, t))
                dve.wait_ge(rstd_made, n + 1)
                nc.vector.tensor_scalar(x1[:, t, :], x1[:, t, :], mv[:, n, 0:1], rstd[:, n, 1:2],
                                        ALU.subtract, ALU.mult).then_inc(finished, 1)

            def hits(c):
                n = (P // G) * CHUNKS[c][3]
                dve.wait_ge(idx_ready, c + 1)
                for j in range(J):
                    if c:
                        dve.wait_ge(hit_used, J * (c - 1) + j + 1)
                    nc.vector.tensor_scalar(hit[:, j, 0:n], idx_rel[:, c % 2, 0:n], float(j), None,
                                            ALU.is_equal).then_inc(hit_ready, 1)

            def w_rest(c):
                hi, lo = weights(c)
                dve.wait_ge(w_hi_ready, c + 1)
                nc.vector.tensor_tensor(lo, bank_of("lut", c)[:, 0:CHUNKS[c][3]], value(hi), ALU.subtract)\
                    .then_inc(w_lo_ready, 1)

            def wp_rest(k):
                dve.wait_ge(wp_hi_ready, k + 1)
                nc.vector.tensor_tensor(wp_lo[:, k, :], wp_in[:, k % 2, :], value(wp_hi[:, k, :]), ALU.subtract)\
                    .then_inc(wp_lo_ready, 1)

            def decoding(c):
                if c + 1 < len(CHUNKS):
                    hits(c + 1)
                w_rest(c)

            for k in range(DT):
                dve.wait_ge(ld[f"xt0_{k}"], 16)
            nc.vector.tensor_copy(xT_hi[:, :, 0:S], xT_sb[:, :, 0:S]).then_inc(xt0_hi_ready, 1)
            dve.wait_ge(xt0_hi_ready, 1)
            nc.vector.tensor_tensor(xT_lo[:, :, 0:S], xT_sb[:, :, 0:S], value(xT_hi[:, :, 0:S]),
                                    ALU.subtract).then_inc(in_lo_ready, 1)
            dve.wait_ge(wx_hi_ready, 1)
            nc.vector.tensor_tensor(wx_lo, wx[:, :, :], value(wx_hi), ALU.subtract).then_inc(in_lo_ready, 1)
            dve.wait_ge(ld["wz"], 16)
            nc.vector.tensor_copy(wz_hi, wz[:, :, :]).then_inc(wz_hi_ready, 1)
            dve.wait_ge(wz_hi_ready, 1)
            nc.vector.tensor_tensor(wz_lo, wz[:, :, :], value(wz_hi), ALU.subtract).then_inc(in_lo_ready, 1)
            dve.wait_ge(ld["ch"], 16)
            for u in range(NH * CT):
                conv_taps(u)
                if u == 1:
                    dve.wait_ge(sel_made, Q)
                    nc.vector.tensor_copy(sel_r[:, :], sel[:, :, :, :].rearrange("p t g n -> p (t g n)"))\
                        .then_inc(sel_ready, 1)
                if u in (1, 2):
                    wp_rest(u - 1)
                if u in (4, 5):
                    wp_rest(u - 2)
            for b in range(NB):
                if b == 2:
                    dve.wait_ge(ld["wo"], 16)
                    nc.vector.tensor_copy(wo_hi[:, :, :], wo_in).then_inc(wo_hi_ready, 1)
                    dve.wait_ge(wo_hi_ready, 1)
                    nc.vector.tensor_tensor(wo_lo[:, :, :], wo_in, value(wo_hi[:, :, :]), ALU.subtract)\
                        .then_inc(wo_lo_ready, 1)
                    dve.wait_ge(wo_lo_ready, 1)
                dve.wait_ge(score_ready, b + 1)
                nc.vector.tensor_scalar(sc[:, LT * b:LT * (b + 1), :],
                                        bank_of("score", b)[:, :].rearrange("p (s l) -> p s l", s=LT),
                                        -SCALE, None, ALU.mult).then_inc(score_copied, 1)
            softplus(0)
            hits(0)
            spread(0)
            hits(1)
            state_in(0)
            w_rest(0)
            state_out(0)
            decoding(1)
            dve.wait_ge(z_ready, NH * CT)
            for a in w_in:
                nc.vector.memset(value(a[:, :, :, I:IP]), 0.0).then_inc(pad_made, 1)
            for m in range(1, CT):
                state_in(m)
                if m == CT - 1:
                    spread(1)
                hits(2 * m + 1)
                w_rest(2 * m)
                state_out(m)
                if m == CT - 2:
                    softplus(1)
                decoding(2 * m + 1)
            dve.wait_ge(ld["x"], 16)
            dve.wait_ge(mask_made, 2 + NB)
            state_space(CT)
            mixed((0, 1))
            state_space(CT + 1)
            mask((0, 1))
            mixed((2, 3))
            state_space(CT + 2)
            attend((0, 1))
            hits(NCH_IN + 1)
            state_in(CT + 3)
            mask((2, 3))
            state_out(CT + 3)
            w_rest(NCH_IN)
            attend((2, 3))
            dve.wait_ge(y_hi_ready, NH * CT)
            nc.vector.tensor_tensor(y_lo[:, CT - 1, :], zs[:, CT - 1, S:T], value(y_hi[:, CT - 1, :]),
                                    ALU.subtract).then_inc(y_last_lo_ready, 1)
            decoding(NCH_IN + 1)
            turn_rest(0)
            turn_rest(1)
            mixed((4, 5))
            turn_rest(2)
            turn_rest(3)
            mixed((6, 7))
            decoding(NCH_IN + 2)
            hidden(0)
            mask(range(TH, NT))
            hidden(1)
            hidden_rest(0)
            hidden(2)
            hidden_rest(1)
            hits(NCH_IN + 4)
            hidden(3)
            hidden_rest(2)
            w_rest(NCH_IN + 3)
            attend((4,))
            hidden(4)
            hidden_rest(3)
            decoding(NCH_IN + 4)
            attend((5,))
            hidden(5)
            hidden_rest(4)
            hidden_rest(5)
            w_rest(NCH_IN + 5)
            attend((6,))
            attend((7,))
            ffn_sum(0)
            ffn_sum(1)
            turn_rest(4)
            turn_rest(5)
            turn_rest(6)
            turn_rest(7)
            ffn_sum(2)
            ffn_sum(3)
            hidden(IT)
            for n in range(IT + 1, NH * IT):
                hidden(n)
                hidden_rest(n - 1)
                if n - IT <= TH:
                    finish(n - IT - 1)
            hidden_rest(NH * IT - 1)
            ffn_sum(TH)
            for t in range(TH + 1, NT):
                ffn_sum(t)
                finish(t - 1)
            finish(NT - 1)


def kernel(**inputs):
    import numpy as np
    import concourse.bacc as bacc
    from concourse import mybir as mb
    from concourse.bass_utils import run_bass_kernel_spmd

    a = {n: np.asarray(v) for n, v in inputs.items()}
    B, L, D = a["x"].shape
    flat = a["x"].reshape(B * L, D)
    pre = "L0_attn_"
    C = a[pre + "W_in_x"].shape[0]
    col = lambda n: a[n].reshape(-1, 1)
    device = {
        "x": flat, "xT": flat.T,
        "WxT": a[pre + "W_in_x"].T, "WzT": a[pre + "W_in_z"].T,
        "chan": np.concatenate([a[pre + "conv_w"].reshape(C, -1), col(pre + "conv_b"), col(pre + "D"),
                                col(pre + "A_log")], axis=1),
        "WpT": a[pre + "W_param"].T, "WdtT": a[pre + "W_dt"].T, "b_dt": col(pre + "b_dt"),
        "WoT": a[pre + "W_out"].T,
        "ctxT": a["ctx_512"].reshape(B * L, -1).T,
        "WqT": a["L0_xattn_Wq"].T, "WkT": a["L0_xattn_Wk"].T,
        "bq": col("L0_xattn_bq"), "bk": col("L0_xattn_bk"),
        "attn_mask": a["mask_SxS2_bk1"], "key_mask": a["mask_BxS2_bf0"],
        "lut": a["L0_ffn_lut"], "gate_idxT": a["L0_ffn_gate_idx"].T, "up_idxT": a["L0_ffn_up_idx"].T,
        "down_idxT": a["L0_ffn_down_idx"].T,
    }
    nc = bacc.Bacc("TRN2", target_bir_lowering=False, num_devices=1)
    arrays, args = {}, []
    for name, v in device.items():
        v = np.ascontiguousarray(v)
        arrays[f"in_{name}"] = v
        args.append(nc.dram_tensor(f"in_{name}", v.shape, mb.dt.from_np(v.dtype), kind="ExternalInput").ap())
    args.append(nc.dram_tensor("out_y", (B * L, D), mb.dt.float32, kind="ExternalOutput").ap())
    post_norm_decoder_layer(nc, *args)
    r = run_bass_kernel_spmd(nc, [arrays], core_ids=[0])
    return r.results[0]["out_y"].reshape(B, L, D)
```
